# Optimizing a Trainium2 kernel written in Bass

```python
import numpy as np
import jax
import jax.numpy as jnp

def _softmax(x, axis=-1):
    return jax.nn.softmax(x, axis=axis)

def _gelu(x):
    return jax.nn.gelu(x, approximate=True)

def _silu(x):
    return jax.nn.silu(x)

def _sigmoid(x):
    return jax.nn.sigmoid(x)

def _layernorm(x, axis=-1, eps=1e-05):
    m = jnp.mean(x, axis=axis, keepdims=True)
    v = jnp.var(x, axis=axis, keepdims=True)
    return (x - m) / jnp.sqrt(v + eps)

def _scatter_add(tgt, idx, src, axis=0):
    return tgt.at[idx].add(src)

def _segment_sum(src, seg, n):
    return jax.ops.segment_sum(src, seg, n)
kernel_name = 'mk_perceiver_d1_seqx_r2_420c5b'

def setup_inputs(seed: int=0):
    np.random.seed(seed)
    _w = jnp.asarray

    def _rec_inputs():
        import jax
        import jax.numpy as jnp
        _rk = jax.random.key(seed)
        x = -9.806e-05 + 1 * jax.random.normal(jax.random.fold_in(_rk, 1), (8, 64, 512), jnp.float32)
        _lenS = 64 - jax.random.randint(jax.random.fold_in(_rk, 7), (8,), 0, max(1, 64 // 4) + 1, jnp.int32)
        _lenS2 = 1601 - jax.random.randint(jax.random.fold_in(_rk, 8), (8,), 0, max(1, 1601 // 4) + 1, jnp.int32)
        _ctx_1024P = jax.random.normal(jax.random.fold_in(_rk, 11), (8, 16, 512), jnp.float32)
        _ctx_1024c = jax.random.dirichlet(jax.random.fold_in(_rk, 511), 0.3 * jnp.ones((16,), jnp.float32), (8, 1601))
        _ctx_1024t = jnp.einsum('bsk,bkd->bsd', _ctx_1024c, _ctx_1024P)
        _ctx_1024t = _ctx_1024t * jax.lax.rsqrt(jnp.mean(jnp.square(_ctx_1024t)) + 1e-12) * 0.953939
        ctx_1024 = -1.52775e-05 + 0.999936 * (_ctx_1024t + 0.3 * jax.random.normal(jax.random.fold_in(_rk, 611), (8, 1601, 512), jnp.float32))
        return (x, ctx_1024)
    x, ctx_1024 = _rec_inputs()

    def _L0_xattn_setup():
        import jax, jax.numpy as jnp
        import numpy as np
        D = 512
        NUM_ITERS = 3
        EPS = 1e-06
        SCALE = D ** (-0.5)

        def rmsnorm(x, w, eps=EPS):
            return x * jax.lax.rsqrt(jnp.mean(x * x, axis=-1, keepdims=True) + eps) * w

        def gru_cell(x, h, wih, whh, bih, bhh):
            gx = x @ wih.T + bih
            gh = h @ whh.T + bhh
            xr, xz, xn = jnp.split(gx, 3, axis=-1)
            hr, hz, hn = jnp.split(gh, 3, axis=-1)
            r = jax.nn.sigmoid(xr + hr)
            z = jax.nn.sigmoid(xz + hz)
            n = jnp.tanh(xn + r * hn)
            return (1.0 - z) * n + z * h
        key = jax.random.key(seed)
        ks = jax.random.split(key, 8)
        B, K, M, d = (8, 64, 2048, D)
        w_std = d ** (-0.5)
        return {'slots': jax.random.normal(ks[0], (B, K, d), jnp.float32), 'P': jax.random.normal(ks[1], (B, M, d), jnp.float32), 'Wq': jax.random.normal(ks[2], (d, d), jnp.float32) * w_std, 'Wk': jax.random.normal(ks[3], (d, d), jnp.float32) * w_std, 'Wv': jax.random.normal(ks[4], (d, d), jnp.float32) * w_std, 'gru_wih': jax.random.normal(ks[5], (3 * d, d), jnp.float32) * w_std, 'gru_whh': jax.random.normal(ks[6], (3 * d, d), jnp.float32) * w_std, 'gru_bih': jnp.zeros((3 * d,), jnp.float32), 'gru_bhh': jnp.zeros((3 * d,), jnp.float32), 'slot_norm_w': jnp.ones((d,), jnp.float32), 'input_norm_w': jnp.ones((d,), jnp.float32)}
    _L0_xattn_all = _L0_xattn_setup()
    _L0_xattn_in = {k: v for k, v in _L0_xattn_all.items() if k in ('Wq', 'Wk', 'Wv', 'gru_wih', 'gru_whh', 'gru_bih', 'gru_bhh', 'slot_norm_w', 'input_norm_w')}
    del _L0_xattn_all

    def _L0_attn_setup():
        import math
        import jax, jax.numpy as jnp
        import numpy as np
        HEADS = 16
        key = jax.random.key(seed)
        k1, k2, k3, k4, k5 = jax.random.split(key, 5)
        B, S, D = (2, 1024, 512)
        return {'x': jax.random.normal(k1, (B, S, D), dtype=jnp.float32), 'Wqkv': jax.random.normal(k2, (3 * D, D), dtype=jnp.float32) * (1.0 / math.sqrt(D)), 'bqkv': jax.random.normal(k3, (3 * D,), dtype=jnp.float32) * 0.02, 'Wo': jax.random.normal(k4, (D, D), dtype=jnp.float32) * (1.0 / math.sqrt(D)), 'bo': jax.random.normal(k5, (D,), dtype=jnp.float32) * 0.02}
    _L0_attn_all = _L0_attn_setup()
    _L0_attn_in = {k: v for k, v in _L0_attn_all.items() if k in ('Wqkv', 'bqkv', 'Wo', 'bo')}
    del _L0_attn_all

    def _L0_ffn_setup():
        import jax, jax.numpy as jnp
        import numpy as np
        BEST_K = 2

        def _expert(xf, w1, w3, w2):
            return jax.nn.silu(xf @ w1) * (xf @ w3) @ w2
        key = jax.random.key(seed)
        ks = jax.random.split(key, 9)
        E, S_sh, D, H = (8, 2, 512, 256)
        B, S = (2, 1024)
        w = lambda k, shape: jax.random.normal(k, shape, dtype=jnp.float32) * 0.02
        return {'x': jax.random.normal(ks[0], (B, S, D), dtype=jnp.float32), 'router_w': w(ks[1], (D, E)), 'router_b': jnp.zeros((E,), dtype=jnp.float32), 'routed_w1': w(ks[2], (E, D, H)), 'routed_w3': w(ks[3], (E, D, H)), 'routed_w2': w(ks[4], (E, H, D)), 'shared_w1': w(ks[5], (S_sh, D, H)), 'shared_w3': w(ks[6], (S_sh, D, H)), 'shared_w2': w(ks[7], (S_sh, H, D))}
    _L0_ffn_all = _L0_ffn_setup()
    _L0_ffn_in = {k: v for k, v in _L0_ffn_all.items() if k in ('router_w', 'router_b', 'routed_w1', 'routed_w3', 'routed_w2', 'shared_w1', 'shared_w3', 'shared_w2')}
    del _L0_ffn_all
    return {'x': x, 'ctx_1024': ctx_1024, 'L0_xattn_Wq': _L0_xattn_in['Wq'], 'L0_xattn_Wk': _L0_xattn_in['Wk'], 'L0_xattn_Wv': _L0_xattn_in['Wv'], 'L0_xattn_gru_wih': _L0_xattn_in['gru_wih'], 'L0_xattn_gru_whh': _L0_xattn_in['gru_whh'], 'L0_xattn_gru_bih': _L0_xattn_in['gru_bih'], 'L0_xattn_gru_bhh': _L0_xattn_in['gru_bhh'], 'L0_xattn_slot_norm_w': _L0_xattn_in['slot_norm_w'], 'L0_xattn_input_norm_w': _L0_xattn_in['input_norm_w'], 'L0_attn_Wqkv': _L0_attn_in['Wqkv'], 'L0_attn_bqkv': _L0_attn_in['bqkv'], 'L0_attn_Wo': _L0_attn_in['Wo'], 'L0_attn_bo': _L0_attn_in['bo'], 'L0_ffn_router_w': _L0_ffn_in['router_w'], 'L0_ffn_router_b': _L0_ffn_in['router_b'], 'L0_ffn_routed_w1': _L0_ffn_in['routed_w1'], 'L0_ffn_routed_w3': _L0_ffn_in['routed_w3'], 'L0_ffn_routed_w2': _L0_ffn_in['routed_w2'], 'L0_ffn_shared_w1': _L0_ffn_in['shared_w1'], 'L0_ffn_shared_w3': _L0_ffn_in['shared_w3'], 'L0_ffn_shared_w2': _L0_ffn_in['shared_w2']}

def reference(x, ctx_1024, L0_xattn_Wq, L0_xattn_Wk, L0_xattn_Wv, L0_xattn_gru_wih, L0_xattn_gru_whh, L0_xattn_gru_bih, L0_xattn_gru_bhh, L0_xattn_slot_norm_w, L0_xattn_input_norm_w, L0_attn_Wqkv, L0_attn_bqkv, L0_attn_Wo, L0_attn_bo, L0_ffn_router_w, L0_ffn_router_b, L0_ffn_routed_w1, L0_ffn_routed_w3, L0_ffn_routed_w2, L0_ffn_shared_w1, L0_ffn_shared_w3, L0_ffn_shared_w2):
    import jax
    import jax.numpy as jnp

    def _L0_xattn_ref(slots, P, Wq, Wk, Wv, gru_wih, gru_whh, gru_bih, gru_bhh, slot_norm_w, input_norm_w):
        import jax, jax.numpy as jnp
        import numpy as np
        D = 512
        NUM_ITERS = 3
        EPS = 1e-06
        SCALE = D ** (-0.5)

        def rmsnorm(x, w, eps=EPS):
            return x * jax.lax.rsqrt(jnp.mean(x * x, axis=-1, keepdims=True) + eps) * w

        def gru_cell(x, h, wih, whh, bih, bhh):
            gx = x @ wih.T + bih
            gh = h @ whh.T + bhh
            xr, xz, xn = jnp.split(gx, 3, axis=-1)
            hr, hz, hn = jnp.split(gh, 3, axis=-1)
            r = jax.nn.sigmoid(xr + hr)
            z = jax.nn.sigmoid(xz + hz)
            n = jnp.tanh(xn + r * hn)
            return (1.0 - z) * n + z * h
        Pn = rmsnorm(P, input_norm_w)
        k_proj = Pn @ Wk.T
        v_proj = Pn @ Wv.T
        for _ in range(NUM_ITERS):
            sn = rmsnorm(slots, slot_norm_w)
            q_proj = sn @ Wq.T
            scores = jnp.einsum('bkd,bmd->bkm', q_proj, k_proj) * SCALE
            attn = jax.nn.softmax(scores, axis=-2)
            attn = attn / (jnp.sum(attn, axis=-1, keepdims=True) + EPS)
            updates = jnp.einsum('bkm,bmd->bkd', attn, v_proj)
            slots = gru_cell(updates, slots, gru_wih, gru_whh, gru_bih, gru_bhh)
        return slots

    def _L0_attn_ref(x, Wqkv, bqkv, Wo, bo):
        import math
        import jax, jax.numpy as jnp
        import numpy as np
        HEADS = 16
        B, S, D = x.shape
        H = HEADS
        hd = D // H
        qkv = x @ Wqkv.T + bqkv
        qkv = qkv.reshape(B, H, S, 3 * hd)
        q, k, v = jnp.split(qkv, 3, axis=-1)
        scores = jnp.einsum('bhsd,bhtd->bhst', q, k) * (1.0 / math.sqrt(hd))
        attn = jax.nn.softmax(scores, axis=-1)
        vals = jnp.einsum('bhst,bhtd->bhsd', attn, v)
        vals = vals.reshape(B, S, D)
        return vals @ Wo.T + bo

    def _L0_ffn_ref(x, router_w, router_b, routed_w1, routed_w3, routed_w2, shared_w1, shared_w3, shared_w2):
        import jax, jax.numpy as jnp
        import numpy as np
        BEST_K = 2

        def _expert(xf, w1, w3, w2):
            return jax.nn.silu(xf @ w1) * (xf @ w3) @ w2
        B, S, D = x.shape
        T = B * S
        xf = x.reshape(T, D)
        logits = xf @ router_w + router_b
        topk_vals, topk_idx = jax.lax.top_k(logits, BEST_K)
        sparse = jnp.full_like(logits, -jnp.inf)
        sparse = sparse.at[jnp.arange(T)[:, None], topk_idx].set(topk_vals)
        gates = jax.nn.softmax(sparse, axis=-1)
        routed = jax.vmap(_expert, in_axes=(None, 0, 0, 0))(xf, routed_w1, routed_w3, routed_w2)
        routed_out = jnp.einsum('etd,te->td', routed, gates)
        shared_out = jax.vmap(_expert, in_axes=(None, 0, 0, 0))(xf, shared_w1, shared_w3, shared_w2).sum(axis=0)
        return (routed_out + shared_out).reshape(B, S, D)
    x = x + _L0_xattn_ref(_layernorm(x, axis=-1), ctx_1024, L0_xattn_Wq, L0_xattn_Wk, L0_xattn_Wv, L0_xattn_gru_wih, L0_xattn_gru_whh, L0_xattn_gru_bih, L0_xattn_gru_bhh, L0_xattn_slot_norm_w, L0_xattn_input_norm_w)
    x = x + _L0_attn_ref(_layernorm(x, axis=-1), L0_attn_Wqkv, L0_attn_bqkv, L0_attn_Wo, L0_attn_bo)
    x = x + _L0_ffn_ref(_layernorm(x, axis=-1), L0_ffn_router_w, L0_ffn_router_b, L0_ffn_routed_w1, L0_ffn_routed_w3, L0_ffn_routed_w2, L0_ffn_shared_w1, L0_ffn_shared_w3, L0_ffn_shared_w2)
    return x

_drawn_inputs = setup_inputs


def setup_inputs(seed=0):
    import zlib

    import numpy as np

    out = dict(_drawn_inputs(seed))
    spreads = {'L0_xattn_gru_bih': (0.0, 0.1),
     'L0_xattn_gru_bhh': (0.0, 0.1),
     'L0_xattn_slot_norm_w': (1.0, 0.6),
     'L0_xattn_input_norm_w': (1.0, 0.2),
     'L0_ffn_router_b': (0.0, 0.8)}
    factors = {'L0_attn_bqkv': 5.486,
     'L0_attn_bo': 3.748,
     'L0_ffn_router_w': 3.407,
     'L0_ffn_routed_w1': 3.013,
     'L0_ffn_routed_w3': 2.958,
     'L0_ffn_routed_w2': 2.958}
    for name, (base, spread) in spreads.items():
        noise = np.random.default_rng([zlib.crc32(name.encode()), seed]).standard_normal(out[name].shape)
        drawn = base * np.exp(spread * noise) if base else spread * noise
        out[name] = jnp.asarray(drawn.astype(out[name].dtype))
    for name, factor in factors.items():
        out[name] = (out[name] * factor).astype(out[name].dtype)
    return out
```

```python
from contextlib import ExitStack

import concourse.bass as bass
from concourse import mybir

F32 = mybir.dt.float32
F16 = mybir.dt.float16
I32 = mybir.dt.int32
ALU = mybir.AluOpType
ACT = mybir.ActivationFunctionType
AX = mybir.AxisListType.X

P = 128
B, K, D, M = 8, 64, 512, 1601
DC = D // P
MT = -(-M // P)
TAIL = M - (MT - 1) * P
LOADS = (MT - 1) // 4
ITERS = 3
PAIRS = B // 2
G3 = 3 * D
GC = G3 // P
ROWS = B * K
RT = ROWS // P
WS = 128.0
AS = 32768.0
SLOT_SCALE = float(D) ** -0.5
RMS_EPS = 1e-6
LN_EPS = 1e-5
HC = 16
HD = D // HC
HG = HC // 4
NJ = 3 * HG
NG = ROWS // 8
GB = 8
HEAD_SCALE = float(HD) ** -0.5
NE, NS = 8, 2
HH = 2
GS = 4.0
MAGIC = 1597463007.0


class Steps:

    def __init__(self, eng, sem):
        self.eng, self.sem, self.base, self.n = eng, sem, 0, 0

    def __call__(self, ins):
        self.n += 1
        ins.then_inc(self.sem, 1)
        return self.n

    def after(self, n):
        self.eng.wait_ge(self.sem, self.base + n)


def rsqrt(dve, st, v, y, t):
    st.after(st(dve.tensor_scalar(y.bitcast(I32), v.bitcast(I32), -0.5, MAGIC, ALU.mult, ALU.add)))
    for _ in range(3):
        st.after(st(dve.tensor_tensor(t, y, y, ALU.mult)))
        st.after(st(dve.scalar_tensor_tensor(t, t, -0.5, v, ALU.mult, ALU.mult)))
        st.after(st(dve.scalar_tensor_tensor(y, t, 1.5, y, ALU.add, ALU.mult)))


def layernorm(dve, st, src, dst, stats, mv, small, ready):
    var, rstd, tmp = (small[:, j] for j in range(3))
    for t in range(RT):
        n = st(dve.bn_stats(stats[:, t], src[:, t]))
    st.after(n)
    for t in range(RT):
        n = st(dve.bn_aggr(mv[:, t], stats[:, t]))
    st.after(n)
    st.after(st(dve.tensor_scalar(var, mv[:, :, 1], LN_EPS, None, ALU.add)))
    rsqrt(dve, st, var, rstd, tmp)
    for t in range(RT):
        dve.tensor_scalar(dst[:, t], src[:, t], mv[:, t, 0:1], rstd[:, t:t + 1], ALU.subtract,
                          ALU.mult).then_inc(ready, 1)


def split_passes(lhs, rhs):
    return [(lhs(0), rhs(0)), (lhs(0), rhs(1)), (lhs(1), rhs(0))]


def prepare_weights(nc, w, c, dram, h0_dram):
    with ExitStack() as ctx:
        def sb(name, shape, dt=F32):
            return ctx.enter_context(nc.sbuf_tensor(name, shape, dt))

        def sem(name):
            return ctx.enter_context(nc.semaphore(name))

        bank = ctx.enter_context(nc.psum_tensor("w_bank", [P, 8, 512], F32))
        xr = sb("xr", [P, RT, D])
        h0 = sb("first_slots", [P, RT, DC, P])
        stats = sb("stats", [P, RT, 6])
        mv = sb("mv", [P, RT, 2])
        small = sb("ln_small", [P, 3, RT])
        wqkv_raw = sb("wqkv_raw", [P, 3, DC, D])
        wqkv_s = sb("wqkv_s", [P, 3, 2, DC, D], F16)
        wih_raw = sb("wih_raw", [P, GC, D])
        wihT = sb("wihT", [P, 2, DC, G3], F16)
        whh_raw = sb("whh_raw", [P, GC, D])
        w_in_row = sb("w_in_row", [P, D])
        vec_rows = sb("vec_rows", [2 * DC + 2 * GC, P])
        vecs = sb("vecs", [P, 2 * DC + 2 * GC])
        w_slot, w_in = vecs[:, 0:DC], vecs[:, DC:2 * DC]
        bih, bhh = vecs[:, 2 * DC:2 * DC + GC], vecs[:, 2 * DC + GC:]
        f32row = sb("f32row", [P, 2, D])

        x_in, small_in, wqk_in, wv_in, wih_in, whh_in = (sem(n) for n in (
            "x_in", "small_in", "wqk_in", "wv_in", "wih_in", "whh_in"))
        consts_done = sem("w_consts_done")
        vecs_turned = sem("vecs_turned")
        vecs_out = sem("vecs_out")
        dve_done = sem("w_dve_done")
        xn_ready = sem("xn_ready")
        xT_done = sem("xT_done")
        h0_ready = sem("h0_ready")
        h0_out = sem("h0_out")
        qkv_split = sem("qkv_split")
        turned = sem("turned")
        turned_hi = sem("turned_hi")
        turned_lo = sem("turned_lo")
        folded = sem("folded")
        folded_f32 = sem("folded_f32")
        folded_hi = sem("folded_hi")
        folded_lo = sem("folded_lo")

        NF = DC + DC * 3
        turned_view = lambda t: bank[:, 4 + t % 4, :].rearrange("p (c g) -> p c g", c=DC)

        def turn_dst(t, part):
            dst = wihT if t < GC else w.whhT
            g = t % GC
            return dst[:, part, :, g * P:(g + 1) * P]

        def fold_dst(f, part):
            if f < DC:
                return w.A[:, part, f, :]
            dc, g = divmod(f - DC, 3)
            return w.Bt[:, part, dc, g * D:(g + 1) * D]

        block = ctx.enter_context(nc.Block())

        @block.sync
        def _(sp):
            sp.dma_start(xr[:], dram.x.rearrange("b k d -> (b k) d").rearrange("(t p) d -> p t d", p=P)).then_inc(x_in, 16)
            sp.dma_start(wqkv_raw[:, 0], dram.Wq.rearrange("(c p) d -> p c d", p=P)).then_inc(wqk_in, 16)
            sp.dma_start(wqkv_raw[:, 1], dram.Wk.rearrange("(c p) d -> p c d", p=P)).then_inc(wqk_in, 16)
            sp.dma_start(wih_raw[:], dram.gru_wih.rearrange("(c p) d -> p c d", p=P)).then_inc(wih_in, 16)
            sp.dma_start(wqkv_raw[:, 2], dram.Wv.rearrange("(c p) d -> p c d", p=P)).then_inc(wv_in, 16)
            sp.dma_start(whh_raw[:], dram.gru_whh.rearrange("(c p) d -> p c d", p=P)).then_inc(whh_in, 16)
            sp.wait_ge(h0_ready, RT)
            sp.dma_start(h0_dram.rearrange("t p n -> p t n"), h0[:].rearrange("p t c r -> p t (c r)")).then_inc(h0_out, 16)
            sp.wait_ge(h0_out, 16)

        @block.gpsimd
        def _(pool):
            pool.memset(c.ident32[:], 0.0).then_inc(consts_done, 1)
            pool.memset(c.ones16[:], 1.0).then_inc(consts_done, 1)
            pool.memset(c.ones32[:], 1.0).then_inc(consts_done, 1)
            pool.wait_ge(consts_done, 3)
            pool.affine_select(out=c.ident32[:], in_=c.ident32[:], compare_op=ALU.not_equal, fill=1.0,
                               base=0, pattern=[[-1, P]], channel_multiplier=1).then_inc(consts_done, 1)
            pool.wait_ge(consts_done, 4)
            pool.tensor_copy(c.ident16[:], c.ident32[:]).then_inc(consts_done, 1)

        @block.scalar
        def _(act):
            act.dma_start(w_in_row[:], dram.input_norm_w.partition_broadcast(P)).then_inc(small_in, 16)
            at = 0
            for src in (dram.slot_norm_w, dram.input_norm_w, dram.gru_bih, dram.gru_bhh):
                rows = src.shape[0] // P
                act.dma_start(vec_rows[at:at + rows, :], src.rearrange("(c p) -> c p", p=P)).then_inc(small_in, 16)
                at += rows
            for t in range(RT):
                act.wait_ge(xT_done, t + 1)
                act.copy(h0[:, t].rearrange("p c r -> p (c r)"), bank[:, t, :]).then_inc(h0_ready, 1)

            def turned_block(t):
                act.wait_ge(turned, t + 1)
                act.activation(turn_dst(t, 0), turned_view(t), ACT.Copy, scale=WS).then_inc(turned_hi, 1)

            def folded_row(f):
                act.wait_ge(folded_f32, f + 1)
                act.copy(fold_dst(f, 0), f32row[:, f % 2]).then_inc(folded_hi, 1)

            for f in range(DC):
                folded_row(f)
            for t in range(GC):
                turned_block(t)
            for f in range(DC, NF):
                folded_row(f)
            for t in range(GC, 2 * GC):
                turned_block(t)

        @block.vector
        def _(dve):
            st = Steps(dve, dve_done)
            dve.wait_ge(x_in, 16)
            layernorm(dve, st, xr, xr, stats, mv, small, xn_ready)

            def split_raw(j):
                src = wqkv_raw[:, j].rearrange("p c d -> p (c d)")
                hi, lo = (wqkv_s[:, j, n].rearrange("p c d -> p (c d)") for n in range(2))
                st.after(st(dve.tensor_scalar(hi, src, WS, None, ALU.mult)))
                dve.scalar_tensor_tensor(lo, src, WS, hi, ALU.mult, ALU.subtract).then_inc(qkv_split, 1)

            def turned_block(t):
                dve.wait_ge(turned_hi, t + 1)
                dve.scalar_tensor_tensor(turn_dst(t, 1), turned_view(t), WS, turn_dst(t, 0), ALU.mult,
                                         ALU.subtract).then_inc(turned_lo, 1)

            def folded_row(f):
                dve.wait_ge(folded, f + 1)
                if f >= 2:
                    dve.wait_ge(folded_hi, f - 1)
                if f < DC:
                    dve.scalar_tensor_tensor(f32row[:, f % 2], bank[:, f % 2, :], w_slot[:, f:f + 1], w_in_row[:],
                                             ALU.mult, ALU.mult).then_inc(folded_f32, 1)
                else:
                    dc = (f - DC) // 3
                    dve.tensor_scalar(f32row[:, f % 2], bank[:, f % 2, :], w_in[:, dc:dc + 1], None,
                                      ALU.mult).then_inc(folded_f32, 1)

            def folded_low(f):
                dve.wait_ge(folded_hi, f + 1)
                dve.tensor_tensor(fold_dst(f, 1), f32row[:, f % 2], fold_dst(f, 0), ALU.subtract).then_inc(folded_lo, 1)

            dve.wait_ge(wqk_in, 32)
            split_raw(0)
            split_raw(1)
            dve.wait_ge(small_in, 80)
            dve.wait_ge(vecs_turned, 1)
            dve.tensor_copy(vecs[:], bank[:, 7, 0:2 * DC + 2 * GC]).then_inc(vecs_out, 1)
            dve.wait_ge(vecs_out, 1)
            st(dve.tensor_scalar(vecs[:, 0:2 * DC], vecs[:, 0:2 * DC], 1.0 / WS, None, ALU.mult))
            st(dve.tensor_tensor(c.b_rz[:], bih[:, 0:8], bhh[:, 0:8], ALU.add))
            st(dve.tensor_copy(c.b_n[:, 0:DC], bhh[:, 8:12]))
            st.after(st(dve.tensor_copy(c.b_n[:, DC:8], bih[:, 8:12])))
            for f in range(DC):
                folded_row(f)
                folded_low(f)
            dve.wait_ge(wv_in, 16)
            split_raw(2)
            for t in range(GC):
                turned_block(t)
            for f in range(DC, NF):
                folded_row(f)
                folded_low(f)
            for t in range(GC, 2 * GC):
                turned_block(t)

        @block.tensor
        def _(pe):
            pe.wait_ge(consts_done, 5)
            for t in range(RT):
                pe.wait_ge(xn_ready, t + 1)
                for dc in range(DC):
                    mm = pe.transpose(bank[:, t, dc * P:(dc + 1) * P], xr[:, t, dc * P:(dc + 1) * P], c.ident32[:])
                mm.then_inc(xT_done, 1)

            def turn(t, raw):
                if t >= 4:
                    pe.wait_ge(turned_lo, t - 3)
                for dc in range(DC):
                    mm = pe.transpose(bank[:, 4 + t % 4, dc * P:(dc + 1) * P], raw[:, t % GC, dc * P:(dc + 1) * P],
                                      c.ident32[:])
                mm.then_inc(turned, 1)

            def fold(f, lhs, rhs):
                if f >= 2:
                    pe.wait_ge(folded_f32, f - 1)
                n = 0
                for ec in range(DC):
                    for a, b in split_passes(lambda i: lhs(i, ec), lambda i: rhs(i, ec)):
                        mm = pe.matmul(bank[:, f % 2, :], a, b, start=(n == 0), stop=(n == 3 * DC - 1))
                        n += 1
                mm.then_inc(folded, 1)

            pe.wait_ge(small_in, 80)
            pe.transpose(bank[:, 7, 0:2 * DC + 2 * GC], vec_rows[:], c.ident32[0:2 * DC + 2 * GC, 0:2 * DC + 2 * GC])\
                .then_inc(vecs_turned, 1)
            pe.wait_ge(qkv_split, 2)
            pe.wait_ge(h0_ready, RT)
            pe.wait_ge(vecs_out, 1)
            for dc in range(DC):
                fold(dc, lambda i, ec: wqkv_s[:, 0, i, ec, dc * P:(dc + 1) * P], lambda i, ec: wqkv_s[:, 1, i, ec, :])
            pe.wait_ge(wih_in, 16)
            for t in range(GC):
                turn(t, wih_raw)
            pe.wait_ge(qkv_split, 3)
            pe.wait_ge(turned_lo, GC)
            for f in range(DC, NF):
                dc, g = divmod(f - DC, 3)
                fold(f, lambda i, ec: wqkv_s[:, 2, i, ec, dc * P:(dc + 1) * P],
                     lambda i, ec: wihT[:, i, ec, g * D:(g + 1) * D])
            pe.wait_ge(whh_in, 16)
            for t in range(GC, 2 * GC):
                turn(t, whh_raw)


def slot_attention(nc, w, c, dram, h0_dram, h_dram):
    with ExitStack() as ctx:
        def sb(name, shape, dt=F32):
            return ctx.enter_context(nc.sbuf_tensor(name, shape, dt))

        def sem(name):
            return ctx.enter_context(nc.semaphore(name))

        def sems(name):
            return [sem(f"{name}{lane}") for lane in range(2)]

        ctxn = [sb(f"ctxn{n}", [P, MT, 2, D], F16) for n in range(2)]
        ctxT = [sb(f"ctxT{n}", [P, MT, 2, DC, P], F16) for n in range(2)]
        tail = [sb(f"tail{n}", [P, D]) for n in range(2)]
        ssq = [sb(f"ssq{n}", [P, MT]) for n in range(2)]
        rrow = [sb(f"rrow{n}", [P, MT]) for n in range(2)]
        rtmp = [sb(f"rtmp{n}", [P, MT]) for n in range(2)]
        h = [sb(f"slots{n}", [P, DC, K]) for n in range(2)]
        hs = [sb(f"hs{n}", [P, 2, DC, K], F16) for n in range(2)]
        qs = [sb(f"qs{n}", [P, 2, DC, K], F16) for n in range(2)]
        us = [sb(f"us{n}", [P, 2, DC, K], F16) for n in range(2)]
        attn = [sb(f"attn{n}", [P, 2, MT, K], F16) for n in range(2)]
        scratch = [sb(f"scratch{n}", [P, 16 * K]) for n in range(2)]
        f32t = [sb(f"f32t{n}", [P, DC, K]) for n in range(2)]
        cand = [sb(f"cand{n}", [P, DC, K]) for n in range(2)]
        small = [sb(f"small{n}", [P, 3, K]) for n in range(2)]
        rowmax = [sb(f"rowmax{n}", [P, MT]) for n in range(2)]
        rowsum = [sb(f"rowsum{n}", [P, MT]) for n in range(2)]

        score = [ctx.enter_context(nc.psum_tensor(f"score{n}", [P, 1024], F32)) for n in range(2)]
        gate = [ctx.enter_context(nc.psum_tensor(f"gate{n}", [P, 2, 512], F32)) for n in range(2)]

        def raw(n, t):
            if t == MT - 1:
                return tail[n][:]
            return ctxT[n][:, t].rearrange("p s c m -> p (s c m)").bitcast(F32)

        e32 = [s[:, 0:MT * K].rearrange("p (t k) -> p t k", k=K) for s in scratch]
        rz = [s[:, 0:512] for s in scratch]
        hn_xn = [s[:, 512:1024] for s in scratch]

        ctx_in = sems("ctx_in")
        h_in = sems("h_in")
        h_out = sems("h_out")
        tail_zero = sem("tail_zero")
        squares = sems("squares")
        tile_split = sems("tile_split")
        tile_turned = sems("tile_turned")
        even_out = sems("even_out")
        odd_out = sems("odd_out")
        h_hi = sems("h_hi")
        h_sq = sems("h_sq")
        h_lo = sems("h_lo")
        q_done = sems("q_done")
        q_split = sems("q_split")
        scored = sems("scored")
        shifted = sems("shifted")
        expd = sems("expd")
        attn_f32 = sems("attn_f32")
        attn_hi = sems("attn_hi")
        attn_lo = sems("attn_lo")
        updated = sems("updated")
        u_split = sems("u_split")
        gated = sems("gated")
        gates_f32 = sems("gates_f32")
        rz_tanh = sems("rz_tanh")
        cand_sum = sems("cand_sum")
        cand_tanh = sems("cand_tanh")
        h_new = sems("h_new")
        dve_done = sem("s_dve_done")

        block = ctx.enter_context(nc.Block())
        EV = (MT + 1) // 2
        OD = MT // 2
        HE = ITERS + 1

        @block.sync
        def _(sp):
            def load_context(pair, n):
                rows = dram.ctx[bass.ds(pair * 2 + n, 1)].rearrange("a m d -> (a m) d")
                for j in range(LOADS):
                    dst = ctxT[n][:, 4 * j:4 * j + 4].rearrange("p t s c m -> p (t s c m)").bitcast(F32)
                    src = rows[4 * P * j:4 * P * (j + 1), :].rearrange("(p t) d -> p (t d)", t=4)
                    sp.dma_start(dst, src).then_inc(ctx_in[n], 16)
                sp.dma_start(tail[n][0:TAIL, :], rows[(MT - 1) * P:M, :]).then_inc(ctx_in[n], 16)

            def load_slots(pair, n):
                src = h0_dram[bass.ds(pair, 1)].rearrange("a p (c r) -> (a p) c r", c=DC)
                sp.dma_start(h[n][:], src[:, :, n * K:(n + 1) * K]).then_inc(h_in[n], 16)

            def store_slots(pair, n):
                dst = h_dram[bass.ds(pair, 1)].rearrange("a p (c r) -> (a p) c r", c=DC)
                sp.dma_start(dst[:, :, n * K:(n + 1) * K], h[n][:]).then_inc(h_out[n], 16)

            sp.wait_ge(tail_zero, 2)
            for n in range(2):
                load_context(0, n)
                load_slots(0, n)
            with sp.Fori(1, PAIRS) as pair:
                for n in range(2):
                    sp.wait_ge(scored[n], pair * ITERS)
                    load_context(pair, n)
                for n in range(2):
                    sp.wait_ge(h_lo[n], pair * HE)
                    sp.wait_ge(h_sq[n], pair * HE)
                    store_slots(pair - 1, n)
                for n in range(2):
                    sp.wait_ge(h_out[n], pair * 16)
                    load_slots(pair, n)
            for n in range(2):
                sp.wait_ge(h_new[n], PAIRS * ITERS)
                store_slots(PAIRS - 1, n)
            for n in range(2):
                sp.wait_ge(h_out[n], PAIRS * 16)

        @block.gpsimd
        def _(pool):
            for n in range(2):
                pool.memset(tail[n][:], 0.0).then_inc(tail_zero, 1)

        @block.scalar
        def _(act):
            def slots_out(n):
                act.copy(hs[n][:, 0], h[n][:]).then_inc(h_hi[n], 1)
                act.activation(hn_xn[n][:, 0:DC * K], h[n][:].rearrange("p c k -> p (c k)"),
                               ACT.Square).then_inc(h_sq[n], 1)

            def square(n, t):
                act.activation(ctxn[n][:, t].rearrange("p s d -> p (s d)").bitcast(F32), raw(n, t), ACT.Square,
                               accum_out=ssq[n][:, t:t + 1]).then_inc(squares[n], 1)

            def even_tile(pair, n, t):
                act.wait_ge(tile_turned[n], pair * MT + t + 1)
                act.copy(ctxT[n][:, t].rearrange("p s c m -> p (s c m)").bitcast(F32),
                         score[n][:, 0:512]).then_inc(even_out[n], 1)

            with act.Fori(0, PAIRS) as pair:
                for n in range(2):
                    act.wait_ge(h_in[n], (pair + 1) * 16)
                    slots_out(n)
                for n in range(2):
                    act.wait_ge(ctx_in[n], (pair + 1) * 16 * (LOADS + 1))
                    for t in range(MT):
                        square(n, t)
                        if n == 1 and t % 2 == 0:
                            even_tile(pair, 0, t)
                for t in range(0, MT, 2):
                    even_tile(pair, 1, t)
                with act.Fori(0, ITERS) as it:
                    step = pair * ITERS + it + 1
                    for n in range(2):
                        act.wait_ge(shifted[n], step)
                        act.activation(e32[n], e32[n], ACT.Exp, scale=SLOT_SCALE).then_inc(expd[n], 1)
                        act.wait_ge(attn_f32[n], step)
                        act.copy(attn[n][:, 0], e32[n]).then_inc(attn_hi[n], 1)
                    for n in range(2):
                        act.wait_ge(gates_f32[n], step)
                        act.activation(rz[n], rz[n], ACT.Tanh, scale=0.5).then_inc(rz_tanh[n], 1)
                        act.wait_ge(cand_sum[n], step)
                        act.activation(cand[n][:], f32t[n][:], ACT.Tanh).then_inc(cand_tanh[n], 1)
                        act.wait_ge(h_new[n], step)
                        slots_out(n)

        @block.vector
        def _(dve):
            PREP = 2 * (1 + 10 + MT)
            STEP = 2 * (1 + 10 + 2) + 2 * (1 + 2) + 2 * 3 + 2 * (1 + 2)
            st = Steps(dve, dve_done)

            def slots_low(n, event):
                dve.wait_ge(h_hi[n], event)
                dve.tensor_tensor(hs[n][:, 1], h[n][:], hs[n][:, 0], ALU.subtract).then_inc(h_lo[n], 1)

            def prepare(pair, n):
                dve.wait_ge(squares[n], (pair + 1) * MT)
                st.after(st(dve.tensor_scalar(ssq[n][:], ssq[n][:], 1.0 / D, RMS_EPS, ALU.mult, ALU.add)))
                rsqrt(dve, st, ssq[n][:], rrow[n][:], rtmp[n][:])
                high = {}
                for t in range(MT + 3):
                    if t < MT:
                        high[t] = st(dve.tensor_scalar(ctxn[n][:, t, 0], raw(n, t), rrow[n][:, t:t + 1], None, ALU.mult))
                    if 1 <= t <= MT:
                        st.after(high[t - 1])
                        dve.scalar_tensor_tensor(ctxn[n][:, t - 1, 1], raw(n, t - 1), rrow[n][:, t - 1:t],
                                                 ctxn[n][:, t - 1, 0], ALU.mult, ALU.subtract).then_inc(tile_split[n], 1)
                    if t >= 3 and t % 2 == 0:
                        dve.wait_ge(tile_turned[n], pair * MT + t - 3 + 1)
                        dve.tensor_copy(ctxT[n][:, t - 3].rearrange("p s c m -> p (s c m)").bitcast(F32),
                                        score[n][:, 512:1024]).then_inc(odd_out[n], 1)

            def q_out(n, step):
                v, y, t = (small[n][:, j] for j in range(3))
                dve.wait_ge(q_done[n], step)
                st.after(st(dve.tensor_scalar(v, score[n][:, 768:832], WS * WS / D, RMS_EPS * WS * WS, ALU.mult, ALU.add)))
                rsqrt(dve, st, v, y, t)
                st.after(st(dve.tensor_tensor(f32t[n][:], score[n][:, 512:768].rearrange("p (c k) -> p c k", c=DC),
                                              y.unsqueeze(1).to_broadcast([P, DC, K]), ALU.mult)))
                st.after(st(dve.tensor_copy(qs[n][:, 0], f32t[n][:])))
                dve.tensor_tensor(qs[n][:, 1], f32t[n][:], qs[n][:, 0], ALU.subtract).then_inc(q_split[n], 1)

            def softmax_shift(n, step):
                s = score[n][:, 0:MT * K].rearrange("p (t k) -> p t k", k=K)
                dve.wait_ge(scored[n], step)
                st.after(st(dve.tensor_reduce(rowmax[n][:], s, AX, ALU.max)))
                dve.tensor_tensor(e32[n], s, rowmax[n][:].unsqueeze(2).to_broadcast([P, MT, K]),
                                  ALU.subtract).then_inc(shifted[n], 1)

            def softmax_norm(n, step):
                dve.wait_ge(expd[n], step)
                st.after(st(dve.tensor_reduce(rowsum[n][:], e32[n], AX, ALU.add)))
                st.after(st(dve.reciprocal(rowsum[n][:], rowsum[n][:])))
                dve.scalar_tensor_tensor(e32[n], e32[n], AS, rowsum[n][:].unsqueeze(2).to_broadcast([P, MT, K]),
                                         ALU.mult, ALU.mult).then_inc(attn_f32[n], 1)

            def softmax_low(n, step):
                dve.wait_ge(attn_hi[n], step)
                dve.tensor_tensor(attn[n][:, 1], e32[n], attn[n][:, 0], ALU.subtract).then_inc(attn_lo[n], 1)

            def update_out(n, step):
                r = small[n][:, 0]
                dve.wait_ge(updated[n], step)
                st.after(st(dve.tensor_scalar(r, score[n][:, 256:320], RMS_EPS * AS, None, ALU.add)))
                st.after(st(dve.reciprocal(r, r)))
                st.after(st(dve.tensor_tensor(f32t[n][:], score[n][:, 0:256].rearrange("p (c k) -> p c k", c=DC),
                                              r.unsqueeze(1).to_broadcast([P, DC, K]), ALU.mult)))
                st.after(st(dve.tensor_copy(us[n][:, 0], f32t[n][:])))
                dve.tensor_tensor(us[n][:, 1], f32t[n][:], us[n][:, 0], ALU.subtract).then_inc(u_split[n], 1)

            def gates_in(n, step):
                dve.wait_ge(gated[n], step)
                for part, dst, bias in ((0, rz[n], c.b_rz), (1, hn_xn[n], c.b_n)):
                    ins = dve.scalar_tensor_tensor(dst.rearrange("p (c k) -> p c k", k=K),
                                                   gate[n][:, part, :].rearrange("p (c k) -> p c k", k=K), 1.0 / WS,
                                                   bias[:].unsqueeze(2).to_broadcast([P, 2 * DC, K]), ALU.mult, ALU.add)
                ins.then_inc(gates_f32[n], 1)

            def candidate(n, step):
                f = f32t[n][:].rearrange("p c k -> p (c k)")
                dve.wait_ge(rz_tanh[n], step)
                st.after(st(dve.scalar_tensor_tensor(f, rz[n][:, 0:256], 1.0, hn_xn[n][:, 0:256], ALU.add, ALU.mult)))
                dve.scalar_tensor_tensor(f, f, 0.5, hn_xn[n][:, 256:512], ALU.mult, ALU.add).then_inc(cand_sum[n], 1)

            def new_slots(n, step):
                hf, nf = (a[n][:].rearrange("p c k -> p (c k)") for a in (h, cand))
                dve.wait_ge(cand_tanh[n], step)
                st.after(st(dve.tensor_tensor(rz[n][:, 0:256], hf, nf, ALU.subtract)))
                st.after(st(dve.scalar_tensor_tensor(rz[n][:, 0:256], rz[n][:, 256:512], 1.0, rz[n][:, 0:256],
                                                     ALU.add, ALU.mult)))
                dve.scalar_tensor_tensor(hf, rz[n][:, 0:256], 0.5, nf, ALU.mult, ALU.add).then_inc(h_new[n], 1)

            with dve.Fori(0, PAIRS) as pair:
                st.base, st.n = pair * (PREP + ITERS * STEP_OWN), 0
                for n in range(2):
                    slots_low(n, pair * HE + 1)
                for n in range(2):
                    prepare(pair, n)
                assert st.n == PREP, st.n
                with dve.Fori(0, ITERS) as it:
                    st.base, st.n = pair * (PREP + ITERS * STEP_OWN) + it * STEP_OWN + PREP, 0
                    step = pair * ITERS + it + 1
                    q_out(0, step)
                    softmax_shift(0, step)
                    q_out(1, step)
                    softmax_norm(0, step)
                    softmax_low(0, step)
                    softmax_shift(1, step)
                    softmax_norm(1, step)
                    update_out(0, step)
                    softmax_low(1, step)
                    gates_in(0, step)
                    candidate(0, step)
                    update_out(1, step)
                    new_slots(0, step)
                    slots_low(0, pair * HE + it + 2)
                    gates_in(1, step)
                    candidate(1, step)
                    new_slots(1, step)
                    slots_low(1, pair * HE + it + 2)
                    assert st.n == STEP_OWN, st.n

        @block.tensor
        def _(pe):
            def turn(pair, n):
                for t in range(MT):
                    pe.wait_ge(tile_split[n], pair * MT + t + 1)
                    if t >= 2:
                        pe.wait_ge(*((odd_out[n], pair * OD + t // 2) if t % 2 else (even_out[n], pair * EV + t // 2)))
                    dst = score[n][:, t % 2 * 512:t % 2 * 512 + 512].bitcast(F16)
                    for j in range(2 * DC):
                        s, dc = divmod(j, DC)
                        mm = pe.transpose(dst[:, j * P:(j + 1) * P], ctxn[n][:, t, s, dc * P:(dc + 1) * P], c.ident16[:])
                    mm.then_inc(tile_turned[n], 1)

            def chunks(dst, weights, operand, start):
                for o in range(len(dst)):
                    for dc in range(DC):
                        for a, b in split_passes(lambda i: weights(i, dc, o), lambda i: operand[:, i, dc]):
                            mm = pe.matmul(dst[o], a, b, start=start, stop=True, skip_group_check=True)
                            start = False
                return mm

            def query(pair, it, n):
                pe.wait_ge(even_out[n], (pair + 1) * EV)
                pe.wait_ge(odd_out[n], (pair + 1) * OD)
                pe.wait_ge(h_sq[n], pair * HE + it + 1)
                for dc in range(DC):
                    pe.matmul(score[n][:, 768:832], c.ones32[:], hn_xn[n][:, dc * K:(dc + 1) * K], start=(dc == 0),
                              stop=True, skip_group_check=True)
                pe.wait_ge(h_hi[n], pair * HE + it + 1)
                pe.wait_ge(h_lo[n], pair * HE + it + 1)
                chunks([score[n][:, 512 + o * K:512 + (o + 1) * K] for o in range(DC)],
                       lambda i, dc, o: w.A[:, i, dc, o * P:(o + 1) * P], hs[n], False).then_inc(q_done[n], 1)

            def gate_cols(n, g):
                return gate[n][:, g // 8, g % 8 * K:(g % 8 + 1) * K]

            def hidden_rz(n):
                chunks([gate_cols(n, g) for g in range(8)], lambda i, dc, o: w.whhT[:, i, dc, o * P:(o + 1) * P],
                       hs[n], True)

            def hidden_n(n):
                chunks([gate_cols(n, 8 + g) for g in range(4)],
                       lambda i, dc, o: w.whhT[:, i, dc, (8 + o) * P:(9 + o) * P], hs[n], True)

            def scores(step, n):
                pe.wait_ge(q_split[n], step)
                for t in range(MT):
                    k = 0
                    for dc in range(DC):
                        for a, b in split_passes(lambda i: ctxT[n][:, t, i, dc], lambda i: qs[n][:, i, dc]):
                            mm = pe.matmul(score[n][:, t * K:(t + 1) * K], a, b, start=(k == 0), stop=(k == 3 * DC - 1),
                                           skip_group_check=True)
                            k += 1
                mm.then_inc(scored[n], 1)

            def update(step, n):
                pe.wait_ge(attn_hi[n], step)
                pe.wait_ge(attn_lo[n], step)
                rows = [P] * (MT - 1) + [TAIL]
                for t in range(MT):
                    for i in range(2):
                        pe.matmul(score[n][:, 256:320], c.ones16[0:rows[t], :], attn[n][0:rows[t], i, t],
                                  start=(t == 0 and i == 0), stop=True, skip_group_check=True)
                for dc in range(DC):
                    for t in range(MT):
                        for a, b in split_passes(lambda i: ctxn[n][0:rows[t], t, i, dc * P:(dc + 1) * P],
                                                 lambda i: attn[n][0:rows[t], i, t]):
                            mm = pe.matmul(score[n][:, dc * K:(dc + 1) * K], a, b, start=False, stop=True,
                                           skip_group_check=True)
                mm.then_inc(updated[n], 1)

            def inputs(step, n):
                pe.wait_ge(u_split[n], step)
                cols = [gate_cols(n, g) for g in range(8)] + [gate_cols(n, 12 + g) for g in range(4)]
                chunks(cols, lambda i, dc, o: w.Bt[:, i, dc, o * P:(o + 1) * P], us[n], False).then_inc(gated[n], 1)

            with pe.Fori(0, PAIRS) as pair:
                for n in range(2):
                    turn(pair, n)
                with pe.Fori(0, ITERS) as it:
                    step = pair * ITERS + it + 1
                    query(pair, it, 0)
                    hidden_rz(0)
                    hidden_n(0)
                    scores(step, 0)
                    query(pair, it, 1)
                    hidden_rz(1)
                    scores(step, 1)
                    update(step, 0)
                    hidden_n(1)
                    inputs(step, 0)
                    update(step, 1)
                    inputs(step, 1)


STEP_OWN = 2 * (1 + 10 + 2) + 2 * 1 + 2 * 2 + 2 * 4 + 2 * 1 + 2 * 2


def project_qkv(nc, c, dram, h_dram, rows, folded):
    with ExitStack() as ctx:
        def sb(name, shape, dt=F32):
            return ctx.enter_context(nc.sbuf_tensor(name, shape, dt))

        def sem(name):
            return ctx.enter_context(nc.semaphore("p_" + name))

        bank = ctx.enter_context(nc.psum_tensor("p_bank", [P, 8, 512], F32))
        hT = sb("p_hT", [P, RT, DC, P])
        xn = hT[:].rearrange("p t c r -> p t (c r)")
        xT = sb("p_xT", [P, 2, DC, ROWS], F16)
        raw = sb("p_raw", [P, NJ, D])
        wT = sb("p_wT", [P, 2, DC, NJ * P], F16)
        bias_rows = sb("p_bias_rows", [NJ, P])
        bias = sb("p_bias", [P, NJ])
        stats = sb("p_stats", [P, RT, 6])
        mv = sb("p_mv", [P, RT, 2])
        small = sb("p_small", [P, 3, RT])

        x_in, h_in, w_in, b_in, h_rows, x_rows, xn_ready, x_turned, x_hi, x_lo, turned, turned_hi, turned_lo, \
            b_turned, b_out, projected, proj_out, moved, dve_done = (sem(n) for n in (
                "x_in", "h_in", "w_in", "b_in", "h_rows", "x_rows", "xn_ready", "x_turned", "x_hi", "x_lo", "turned",
                "turned_hi", "turned_lo", "b_turned", "b_out", "projected", "proj_out", "moved", "dve_done"))
        w_rows = dram.Wqkv.rearrange("(i ii s e) d -> ii s e i d", i=HG, ii=4, s=3)
        b_rows = dram.bqkv.rearrange("(i ii s e) -> s i ii e", i=HG, ii=4, s=3)

        block = ctx.enter_context(nc.Block())

        @block.sync
        def _(sp):
            sp.dma_start(rows[:], dram.x.rearrange("b k d -> (b k) d").rearrange("(t p) d -> p t d", p=P)).then_inc(x_in, 16)
            sp.dma_start(hT[:].rearrange("p t c r -> p t (c r)"), h_dram.rearrange("t p n -> p t n")).then_inc(h_in, 16)
            for s in range(3):
                for ii in range(4):
                    sp.dma_start(raw[32 * ii:32 * ii + 32, HG * s:HG * s + HG, :], w_rows[ii, s]).then_inc(w_in, 16)
            for s in range(3):
                sp.wait_ge(proj_out, HG * (s + 1))
                for ii in range(4):
                    sp.dma_start(folded[s][:, ii:HC:4, :], raw[32 * ii:32 * ii + 32, HG * s:HG * s + HG, :]).then_inc(moved, 16)
            sp.wait_ge(moved, 12 * 16)

        @block.scalar
        def _(act):
            for s in range(3):
                act.dma_start(bias_rows[HG * s:HG * s + HG, :].rearrange("i (ii e) -> i ii e", ii=4),
                              b_rows[s]).then_inc(b_in, 16)
            for j in range(NJ):
                act.wait_ge(turned, j + 1)
                act.activation(wT[:, 0, :, j * P:(j + 1) * P], bank[:, 4 + j % 4, :].rearrange("p (c g) -> p c g", c=DC),
                               ACT.Copy, scale=WS).then_inc(turned_hi, 1)
            for t in range(RT):
                act.wait_ge(x_turned, t + 1)
                act.copy(xT[:, 0, :, t * P:(t + 1) * P], bank[:, t, :].rearrange("p (c r) -> p c r", c=DC)).then_inc(x_hi, 1)
            act.wait_ge(b_out, 1)
            for j in range(NJ):
                act.wait_ge(projected, j + 1)
                act.activation(raw[:, j, :], bank[:, 4 + j % 4, :], ACT.Identity, bias=bias[:, j:j + 1],
                               scale=1.0 / WS).then_inc(proj_out, 1)

        @block.vector
        def _(dve):
            st = Steps(dve, dve_done)
            dve.wait_ge(x_in, 16)
            for t in range(RT):
                dve.wait_ge(h_rows, t + 1)
                dve.tensor_tensor(rows[:, t], bank[:, t, :], rows[:, t], ALU.add).then_inc(x_rows, 1)
            dve.wait_ge(x_rows, RT)
            layernorm(dve, st, rows, xn, stats, mv, small, xn_ready)
            for j in range(NJ):
                dve.wait_ge(turned_hi, j + 1)
                dve.scalar_tensor_tensor(wT[:, 1, :, j * P:(j + 1) * P], bank[:, 4 + j % 4, :].rearrange("p (c g) -> p c g", c=DC),
                                         WS, wT[:, 0, :, j * P:(j + 1) * P], ALU.mult, ALU.subtract).then_inc(turned_lo, 1)
            for t in range(RT):
                dve.wait_ge(x_hi, t + 1)
                dve.tensor_tensor(xT[:, 1, :, t * P:(t + 1) * P], bank[:, t, :].rearrange("p (c r) -> p c r", c=DC),
                                  xT[:, 0, :, t * P:(t + 1) * P], ALU.subtract).then_inc(x_lo, 1)
            dve.wait_ge(b_turned, 1)
            dve.tensor_copy(bias[:], bank[:, 0, 0:NJ]).then_inc(b_out, 1)

        @block.tensor
        def _(pe):
            pe.wait_ge(h_in, 16)
            for t in range(RT):
                for dc in range(DC):
                    mm = pe.transpose(bank[:, t, dc * P:(dc + 1) * P], hT[:, t, dc], c.ident32[:])
                mm.then_inc(h_rows, 1)
            pe.wait_ge(w_in, 12 * 16)
            for j in range(NJ):
                if j >= 4:
                    pe.wait_ge(turned_lo, j - 3)
                for dc in range(DC):
                    mm = pe.transpose(bank[:, 4 + j % 4, dc * P:(dc + 1) * P], raw[:, j, dc * P:(dc + 1) * P], c.ident32[:])
                mm.then_inc(turned, 1)
            for t in range(RT):
                pe.wait_ge(xn_ready, t + 1)
                for dc in range(DC):
                    mm = pe.transpose(bank[:, t, dc * P:(dc + 1) * P], xn[:, t, dc * P:(dc + 1) * P], c.ident32[:])
                mm.then_inc(x_turned, 1)
            pe.wait_ge(x_lo, RT)
            pe.wait_ge(b_in, 48)
            pe.transpose(bank[:, 0, 0:NJ], bias_rows[:], c.ident32[0:NJ, 0:NJ]).then_inc(b_turned, 1)
            pe.wait_ge(turned_lo, NJ)
            for j in range(NJ):
                if j >= 4:
                    pe.wait_ge(proj_out, j - 3)
                n = 0
                for dc in range(DC):
                    for a, b in split_passes(lambda i: wT[:, i, dc, j * P:(j + 1) * P], lambda i: xT[:, i, dc, :]):
                        mm = pe.matmul(bank[:, 4 + j % 4, :], a, b, start=(n == 0), stop=(n == 3 * DC - 1))
                        n += 1
                mm.then_inc(projected, 1)


def head_attention(nc, c, dram, rows, folded):
    qT, kT, vT = folded
    with ExitStack() as ctx:
        def sb(name, shape, dt=F32):
            return ctx.enter_context(nc.sbuf_tensor(name, shape, dt))

        def sem(name):
            return ctx.enter_context(nc.semaphore("t_" + name))

        score = ctx.enter_context(nc.psum_tensor("t_score", [P, 2, 512], F32))
        probT = ctx.enter_context(nc.psum_tensor("t_probT", [P, 2, 512], F32))
        value = ctx.enter_context(nc.psum_tensor("t_value", [P, 2, 512], F32))
        yb = ctx.enter_context(nc.psum_tensor("t_y", [P, 512], F32))
        vb = ctx.enter_context(nc.psum_tensor("t_vb", [P, 512], F32))
        q_heads = sb("t_q_heads", [HD, 2, 2 * GB, 64])
        v_heads = sb("t_v_heads", [HD, 2, GB, P])
        v = sb("t_v", [P, 2, GB, HD])
        e = sb("t_e", [P, 2, GB, 64])
        stat = sb("t_stat", [P, 2, 2, GB])
        prob = sb("t_prob", [P, 2, GB, P])
        pT = sb("t_pT", [P, 2, GB, P])
        vals = vT
        valsT = sb("t_valsT", [P, DC, ROWS])
        valsS = sb("t_valsS", [P, 2, DC, ROWS], F16)
        wo_raw = sb("t_wo_raw", [P, DC, D])
        woT = sb("t_woT", [P, 2, DC, D], F16)
        bo_row = sb("t_bo_row", [P, D])

        wo_in, bo_in, zeroed, q_ready, v_ready, v_turned, v_out, scored, shifted, expd, prob_out, prob_turned, pT_out, valued, vals_out, \
            wo_turned, wo_hi, wo_lo, vals_hi, vals_lo, y_done, y_out, bo_added, dve_done = (sem(n) for n in (
                "wo_in", "bo_in", "zeroed", "q_ready", "v_ready", "v_turned", "v_out", "scored", "shifted", "expd", "prob_out", "prob_turned",
                "pT_out", "valued", "vals_out", "wo_turned", "wo_hi", "wo_lo", "vals_hi", "vals_lo", "y_done",
                "y_out", "bo_added", "dve_done"))

        moved = [sem(f"moved{t}") for t in range(RT)]

        block = ctx.enter_context(nc.Block())

        @block.sync
        def _(sp):
            sp.dma_start(wo_raw[:], dram.Wo.rearrange("(c p) d -> p c d", p=P)).then_inc(wo_in, 16)
            sp.dma_start(bo_row[:], dram.bo.partition_broadcast(P)).then_inc(bo_in, 16)
            for t in range(RT):
                sp.wait_ge(vals_out, 4 * (t + 1))
                for ii in range(4):
                    sp.dma_start(valsT[32 * ii:32 * ii + 32, :, t * P:(t + 1) * P],
                                 vals[:, ii:HC:4, t * P:(t + 1) * P]).then_inc(moved[t], 16)

        @block.gpsimd
        def _(pool):
            pool.memset(prob[:], 0.0).then_inc(zeroed, 1)

        @block.scalar
        def _(act):
            def heads(k):
                if k >= 2:
                    act.wait_ge(scored, k - 1)
                    act.wait_ge(v_turned, k - 1)
                t = slice(64 * k, 64 * k + 64)
                act.copy(q_heads[:, k % 2].rearrange("e m (c r) -> e m c r", r=4),
                         qT[:, :, t].rearrange("e c (m r) -> e m c r", r=4)).then_inc(q_ready, 1)
                act.copy(v_heads[:, k % 2].rearrange("e g (h c r) -> e (g h) c r", h=2, r=4),
                         vT[:, :, t].rearrange("e c (m r) -> e m c r", r=4)).then_inc(v_ready, 1)

            def v_in(k):
                act.wait_ge(v_turned, k + 1)
                if k >= 2:
                    act.wait_ge(valued, 2 * (k - 1))
                act.copy(v[:, k % 2].rearrange("p g e -> p (g e)"), vb[:, 0:GB * HD]).then_inc(v_out, 1)

            heads(0)
            for i in range(DC):
                act.wait_ge(wo_turned, i + 1)
                act.activation(woT[:, 0, :, i * P:(i + 1) * P], yb[:].rearrange("p (c g) -> p c g", c=DC),
                               ACT.Copy, scale=WS).then_inc(wo_hi, 1)

            def probs_turned(k):
                for j in range(2):
                    act.wait_ge(prob_turned, 2 * k + j + 1)
                    if k >= 2:
                        act.wait_ge(valued, 2 * (k - 1))
                    act.copy(pT[:, k % 2, 4 * j:4 * j + 4, :].rearrange("p g q -> p (g q)"), probT[:, j, :]).then_inc(pT_out, 1)

            def vals_high(t):
                act.wait_ge(moved[t], 64)
                act.copy(valsS[:, 0, :, t * P:(t + 1) * P], valsT[:, :, t * P:(t + 1) * P]).then_inc(vals_hi, 1)

            for k in range(B):
                if k + 1 < B:
                    heads(k + 1)
                act.wait_ge(shifted, k + 1)
                ek = e[:, k % 2].rearrange("p g k -> p (g k)")
                act.activation(ek, ek, ACT.Exp, scale=HEAD_SCALE).then_inc(expd, 1)
                if k >= 1:
                    probs_turned(k - 1)
                v_in(k)
                if k >= 3 and k % 2 == 1:
                    vals_high(k // 2 - 1)
            probs_turned(B - 1)
            vals_high(RT - 1)

        @block.vector
        def _(dve):
            st = Steps(dve, dve_done)
            for i in range(DC):
                dve.wait_ge(wo_hi, i + 1)
                dve.scalar_tensor_tensor(woT[:, 1, :, i * P:(i + 1) * P], yb[:].rearrange("p (c g) -> p c g", c=DC),
                                         WS, woT[:, 0, :, i * P:(i + 1) * P], ALU.mult, ALU.subtract).then_inc(wo_lo, 1)
            dve.wait_ge(bo_in, 16)
            for t in range(RT):
                dve.tensor_tensor(rows[:, t], rows[:, t], bo_row[:], ALU.add).then_inc(bo_added, 1)

            def shift(k):
                s = score[:, k % 2, :].rearrange("p (g k) -> p g k", k=64)
                dve.wait_ge(scored, k + 1)
                st.after(st(dve.tensor_reduce(stat[:, k % 2, 0], s, AX, ALU.max)))
                dve.tensor_tensor(e[:, k % 2], s, stat[:, k % 2, 0].unsqueeze(2).to_broadcast([P, GB, 64]),
                                  ALU.subtract).then_inc(shifted, 1)

            def norm(k):
                dve.wait_ge(expd, k + 1)
                total = stat[:, k % 2, 1]
                st.after(st(dve.tensor_reduce(total, e[:, k % 2], AX, ALU.add)))
                st.after(st(dve.reciprocal(total, total)))
                if k >= 2:
                    dve.wait_ge(prob_turned, 2 * (k - 1))
                if k == 0:
                    dve.wait_ge(zeroed, 1)
                for g in range(2):
                    half = slice(64 * g, 64 * g + 64)
                    ins = dve.tensor_tensor(prob[half, k % 2, :, half], e[half, k % 2],
                                            total[half].unsqueeze(2).to_broadcast([64, GB, 64]), ALU.mult)
                    ins.then_inc(prob_out, 1)

            def values_out(k):
                for j in range(2):
                    dve.wait_ge(valued, 2 * k + j + 1)
                    t0 = 64 * k + 32 * j
                    dst = vals[:, :, t0:t0 + 32].rearrange("e c (m r) -> e m c r", r=4)
                    dve.tensor_copy(dst, value[0:HD, j, :].rearrange("e (m c r) -> e m c r", c=HC, r=4)).then_inc(vals_out, 1)

            def vals_low(t):
                dve.wait_ge(vals_hi, t + 1)
                dve.tensor_tensor(valsS[:, 1, :, t * P:(t + 1) * P], valsT[:, :, t * P:(t + 1) * P],
                                  valsS[:, 0, :, t * P:(t + 1) * P], ALU.subtract).then_inc(vals_lo, 1)

            def add_y(t):
                dve.wait_ge(y_done, t + 1)
                dve.wait_ge(bo_added, RT)
                dve.scalar_tensor_tensor(rows[:, t], yb[:], 1.0 / WS, rows[:, t], ALU.mult, ALU.add).then_inc(y_out, 1)

            for k in range(B):
                shift(k)
                if k >= 1:
                    values_out(k - 1)
                if k >= 3 and k % 2 == 1:
                    vals_low(k // 2 - 1)
                if k >= 4 and k % 2 == 0:
                    add_y(k // 2 - 2)
                norm(k)
            values_out(B - 1)
            add_y(RT - 2)
            vals_low(RT - 1)
            add_y(RT - 1)

        @block.tensor
        def _(pe):
            pe.wait_ge(wo_in, 16)
            for i in range(DC):
                if i >= 1:
                    pe.wait_ge(wo_lo, i)
                for dc in range(DC):
                    mm = pe.transpose(yb[:, dc * P:(dc + 1) * P], wo_raw[:, i, dc * P:(dc + 1) * P], c.ident32[:])
                mm.then_inc(wo_turned, 1)

            def turn_v(k):
                pe.wait_ge(v_ready, k + 1)
                if k >= 1:
                    pe.wait_ge(v_out, k)
                for g in range(GB):
                    mm = pe.transpose(vb[:, g * HD:(g + 1) * HD], v_heads[:, k % 2, g, :], c.ident32[0:HD, 0:HD])
                mm.then_inc(v_turned, 1)

            def scores(k):
                pe.wait_ge(q_ready, k + 1)
                if k >= 2:
                    pe.wait_ge(shifted, k - 1)
                for g in range(GB):
                    for hd in range(2):
                        t0 = 64 * k + 8 * g + 4 * hd
                        mm = pe.matmul(score[64 * hd:64 * hd + 64, k % 2, g * 64:(g + 1) * 64], q_heads[:, k % 2, 2 * g + hd, :],
                                       kT[:, :, t0:t0 + 4], start=True, stop=True)
                mm.then_inc(scored, 1)

            def turn_probs(k):
                pe.wait_ge(prob_out, 2 * (k + 1))
                for j in range(2):
                    if k >= 1:
                        pe.wait_ge(pT_out, 2 * (k - 1) + j + 1)
                    for g in range(4):
                        mm = pe.transpose(probT[:, j, g * P:(g + 1) * P], prob[:, k % 2, 4 * j + g, :], c.ident32[:])
                    mm.then_inc(prob_turned, 1)

            def values(k):
                pe.wait_ge(v_out, k + 1)
                for j in range(2):
                    pe.wait_ge(pT_out, 2 * k + j + 1)
                    if k >= 1:
                        pe.wait_ge(vals_out, 2 * (k - 1) + j + 1)
                    for g in range(4):
                        mm = pe.matmul(value[0:HD, j, g * P:(g + 1) * P], v[:, k % 2, 4 * j + g, :],
                                       pT[:, k % 2, 4 * j + g, :], start=True, stop=True)
                    mm.then_inc(valued, 1)

            def project(t):
                pe.wait_ge(vals_lo, t + 1)
                if t >= 1:
                    pe.wait_ge(y_out, t)
                n = 0
                for dc in range(DC):
                    for a, b in split_passes(lambda i: valsS[:, i, dc, t * P:(t + 1) * P], lambda i: woT[:, i, dc, :]):
                        mm = pe.matmul(yb[:], a, b, start=(n == 0), stop=(n == 3 * DC - 1))
                        n += 1
                mm.then_inc(y_done, 1)

            pe.wait_ge(wo_lo, DC)
            scores(0)
            for k in range(B):
                if k + 1 < B:
                    scores(k + 1)
                turn_v(k)
                turn_probs(k)
                values(k)
                if k >= 3 and k % 2 == 1:
                    project(k // 2 - 1)
            project(RT - 1)


def experts(nc, c, dram, rows, out):
    with ExitStack() as ctx:
        def sb(name, shape, dt=F32):
            return ctx.enter_context(nc.sbuf_tensor(name, shape, dt))

        def sem(name):
            return ctx.enter_context(nc.semaphore("e_" + name))

        yb = ctx.enter_context(nc.psum_tensor("e_y", [P, RT, D], F32))
        hid = ctx.enter_context(nc.psum_tensor("e_hid", [P, 2, HH, ROWS], F32))
        xn = sb("e_xn", [P, RT, D])
        xT = sb("e_xT", [P, DC, ROWS])
        xs = sb("e_xs", [P, 2, DC, ROWS], F16)
        stats = sb("e_stats", [P, RT, 6])
        mv = sb("e_mv", [P, RT, 2])
        small = sb("e_small", [P, 3, RT])
        rw = sb("e_rw", [P, DC, NE])
        rb_row = sb("e_rb_row", [P, NE])
        rank = sb("e_rank", [P, NE])
        lg = sb("e_lg", [P, RT, NE])
        key = sb("e_key", [P, RT, NE])
        pick1 = sb("e_pick1", [P, RT, NE])
        pick2 = sb("e_pick2", [P, RT, NE])
        rest = sb("e_rest", [P, RT, NE])
        col = sb("e_col", [P, 4, RT])
        gT = sb("e_gT", [NE, ROWS])
        sel = sb("e_sel", [NE, NE, P])
        gate_row = sb("e_gate_row", [P, NE, ROWS])
        raw = sb("e_raw", [P, 2, 3, 1024])
        ws = sb("e_ws", [P, 2, 2, 3, 1024], F16)
        th = sb("e_th", [P, HH * ROWS])
        gs = sb("e_gs", [P, 2, 2, HH, ROWS], F16)

        x_ready, x_turned, x_out, x_hi, x_lo, r_in, routed, router_out, gexp_in, gexp_out, gates_out, g_turned, gT_out, \
            spread, spread_out, w_hi, w_lo, hid_done, tanhd, hid_read, g_f32, g_hi, g_lo, y_done, y_out, o_out, \
            consts, dve_done = (sem(n) for n in (
                "x_ready", "x_turned", "x_out", "x_hi", "x_lo", "r_in", "routed", "router_out", "gexp_in", "gexp_out",
                "gates_out", "g_turned", "gT_out", "spread", "spread_out", "w_hi", "w_lo", "hid_done", "tanhd",
                "hid_read", "g_f32", "g_hi", "g_lo", "y_done", "y_out", "o_out", "consts", "dve_done"))

        w_in = [sem(f"w_in{slot}") for slot in range(2)]

        def experts_in_turn(eng, body, between):
            for n in range(NS):
                body(n, n % 2, n, False, 1)
            with eng.Fori(0, NE // 2) as i:
                between(i)
                for u in range(2):
                    body(NS + 2 * i + u, (NS + u) % 2, 2 * i + u, True, i + 2)

        block = ctx.enter_context(nc.Block())

        @block.sync
        def _(sp):
            sp.dma_start(rw[:], dram.router_w.rearrange("(c p) n -> p c n", p=P)).then_inc(r_in, 16)
            sp.dma_start(rb_row[:], dram.router_b.partition_broadcast(P)).then_inc(r_in, 16)

            def load(n, slot, ex, is_routed, uses):
                if not isinstance(n, int):
                    sp.wait_ge(w_lo, n - 1)
                for j, a in enumerate((dram.routed if is_routed else dram.shared)):
                    src = a[bass.ds(ex, 1)].rearrange("a (c p) n -> (a p) c n", p=P)
                    sp.dma_start(raw[:, slot, j].rearrange("p (c n) -> p c n", c=src.shape[1]), src).then_inc(w_in[slot], 16)

            experts_in_turn(sp, load, lambda i: None)
            for t in range(RT):
                sp.wait_ge(y_out, t + 1)
                sp.dma_start(out.rearrange("b k d -> (b k) d")[t * P:(t + 1) * P, :], rows[:, t]).then_inc(o_out, 16)
            sp.wait_ge(o_out, 16 * RT)

        @block.gpsimd
        def _(pool):
            for n in range(NE):
                pool.memset(rank[:, n:n + 1], float(NE - n)).then_inc(consts, 1)

        @block.scalar
        def _(act):
            for t in range(RT):
                act.wait_ge(x_turned, t + 1)
                act.copy(xT[:, :, t * P:(t + 1) * P], yb[:, t, :].rearrange("p (c r) -> p c r", c=DC)).then_inc(x_out, 1)
            act.wait_ge(x_out, RT)
            act.copy(xs[:, 0], xT[:]).then_inc(x_hi, 1)
            act.wait_ge(gexp_in, 1)
            act.activation(lg[:], lg[:], ACT.Exp).then_inc(gexp_out, 1)
            act.wait_ge(g_turned, 1)
            act.copy(gT[:], yb[0:NE, 1, :]).then_inc(gT_out, 1)
            for n in range(NE):
                act.wait_ge(spread, n + 1)
                act.activation(gate_row[:, n], hid[:, n // 2 % 2, n % 2, :], ACT.Copy,
                               scale=0.5 * GS / (WS * WS)).then_inc(spread_out, 1)

            def expert(n, slot, ex, is_routed, uses):
                act.wait_ge(w_in[slot], uses * 48)
                if not isinstance(n, int):
                    act.wait_ge(y_done, n - 1)
                act.activation(ws[:, slot, 0], raw[:, slot], ACT.Copy, scale=WS).then_inc(w_hi, 1)
                act.wait_ge(hid_done, n + 1)
                act.activation(th[:], hid[:, 0].rearrange("p c t -> p (c t)"), ACT.Tanh, scale=0.5 / WS).then_inc(tanhd, 1)
                act.wait_ge(g_f32, n + 1)
                act.copy(gs[:, slot, 0], th[:].rearrange("p (c t) -> p c t", c=HH)).then_inc(g_hi, 1)

            experts_in_turn(act, expert, lambda i: None)

        @block.vector
        def _(dve):
            st = Steps(dve, dve_done)
            layernorm(dve, st, rows, xn, stats, mv, small, x_ready)
            dve.wait_ge(x_hi, 1)
            dve.tensor_tensor(xs[:, 1], xT[:], xs[:, 0], ALU.subtract).then_inc(x_lo, 1)
            st(dve.tensor_copy(sel[:], c.ident32[0:NE, 0:NE].unsqueeze(2).to_broadcast([NE, NE, P])))
            dve.wait_ge(r_in, 32)
            dve.wait_ge(routed, 1)
            dve.wait_ge(consts, NE)
            def wide(a):
                return a.unsqueeze(2).to_broadcast([P, RT, NE])

            ranks = rank[:].unsqueeze(1).to_broadcast([P, RT, NE])
            st.after(st(dve.tensor_tensor(lg[:], yb[:, 0, 0:RT * NE].rearrange("p (t n) -> p t n", n=NE),
                                          rb_row[:].unsqueeze(1).to_broadcast([P, RT, NE]), ALU.add)))

            def first_largest(values, largest, pick):
                st.after(st(dve.tensor_reduce(largest, values, AX, ALU.max)))
                st.after(st(dve.tensor_tensor(key[:], values, wide(largest), ALU.is_equal)))
                st.after(st(dve.tensor_tensor(key[:], key[:], ranks, ALU.mult)))
                st.after(st(dve.tensor_reduce(col[:, 3], key[:], AX, ALU.max)))
                st.after(st(dve.tensor_tensor(pick, key[:], wide(col[:, 3]), ALU.is_equal)))

            first_largest(lg[:], col[:, 0], pick1[:])
            st.after(st(dve.scalar_tensor_tensor(rest[:], pick1[:], -1e30, lg[:], ALU.mult, ALU.add)))
            first_largest(rest[:], col[:, 1], pick2[:])
            st.after(st(dve.tensor_tensor(pick1[:], pick1[:], pick2[:], ALU.add)))
            dve.tensor_tensor(lg[:], lg[:], wide(col[:, 0]), ALU.subtract).then_inc(gexp_in, 1)
            dve.wait_ge(gexp_out, 1)
            st.after(st(dve.tensor_tensor(lg[:], lg[:], pick1[:], ALU.mult)))
            st.after(st(dve.tensor_reduce(col[:, 2], lg[:], AX, ALU.add)))
            st.after(st(dve.reciprocal(col[:, 2], col[:, 2])))
            dve.tensor_tensor(lg[:], lg[:], wide(col[:, 2]), ALU.mult).then_inc(gates_out, 1)
            before = st.n

            def expert(n, slot, ex, is_routed, uses):
                dve.wait_ge(w_hi, n + 1)
                dve.scalar_tensor_tensor(ws[:, slot, 1], raw[:, slot], WS, ws[:, slot, 0], ALU.mult,
                                         ALU.subtract).then_inc(w_lo, 1)
                dve.wait_ge(tanhd, n + 1)
                h1, h3 = (hid[:, j].rearrange("p c t -> p (c t)") for j in range(2))
                st.after(st(dve.scalar_tensor_tensor(th[:], th[:], 1.0, h1, ALU.add, ALU.mult)))
                if is_routed:
                    dve.tensor_tensor(th[:], th[:], h3, ALU.mult).then_inc(hid_read, 1)
                    dve.wait_ge(hid_read, n + 1)
                    gr = gate_row[:, bass.ds(ex, 1)].rearrange("p a t -> p (a t)").unsqueeze(1).to_broadcast([P, HH, ROWS])
                    dve.tensor_tensor(th[:].rearrange("p (c t) -> p c t", c=HH), th[:].rearrange("p (c t) -> p c t", c=HH),
                                      gr, ALU.mult).then_inc(g_f32, 1)
                else:
                    dve.scalar_tensor_tensor(th[:], th[:], 0.5 * GS / (WS * WS), h3, ALU.mult, ALU.mult).then_inc(hid_read, 1)
                    dve.wait_ge(hid_read, n + 1)
                    dve.nop().then_inc(g_f32, 1)
                dve.wait_ge(g_hi, n + 1)
                dve.tensor_tensor(gs[:, slot, 1], th[:].rearrange("p (c t) -> p c t", c=HH), gs[:, slot, 0],
                                  ALU.subtract).then_inc(g_lo, 1)

            def between(i):
                st.base, st.n = before + NS + 2 * i, 0

            experts_in_turn(dve, expert, between)
            for t in range(RT):
                dve.wait_ge(y_done, NS + NE)
                dve.scalar_tensor_tensor(rows[:, t], yb[:, t, :], 1.0 / (WS * GS), rows[:, t], ALU.mult,
                                         ALU.add).then_inc(y_out, 1)

        @block.tensor
        def _(pe):
            for t in range(RT):
                pe.wait_ge(x_ready, t + 1)
                for dc in range(DC):
                    mm = pe.transpose(yb[:, t, dc * P:(dc + 1) * P], xn[:, t, dc * P:(dc + 1) * P], c.ident32[:])
                mm.then_inc(x_turned, 1)
            pe.wait_ge(x_out, RT)
            pe.wait_ge(r_in, 32)
            for t in range(RT):
                for dc in range(DC):
                    mm = pe.matmul(yb[:, 0, t * NE:(t + 1) * NE], xT[:, dc, t * P:(t + 1) * P], rw[:, dc],
                                   start=(dc == 0), stop=(dc == DC - 1))
            mm.then_inc(routed, 1)
            pe.wait_ge(gates_out, 1)
            for t in range(RT):
                mm = pe.transpose(yb[0:NE, 1, t * P:(t + 1) * P], lg[:, t], c.ident32[:])
            mm.then_inc(g_turned, 1)
            pe.wait_ge(gT_out, 1)
            for n in range(NE):
                if n >= 4:
                    pe.wait_ge(spread_out, n - 3)
                pe.matmul(hid[:, n // 2 % 2, n % 2, :], sel[:, n, :], gT[:], start=True, stop=True).then_inc(spread, 1)

            def hidden(n, slot):
                pe.wait_ge(w_hi, n + 1)
                pe.wait_ge(w_lo, n + 1)
                if not (isinstance(n, int) and n == 0):
                    pe.wait_ge(hid_read, n)
                for j in range(2):
                    for hc in range(HH):
                        k = 0
                        for dc in range(DC):
                            at = dc * HH * P + hc * P
                            for a, b in split_passes(lambda i: ws[:, slot, i, j, at:at + P], lambda i: xs[:, i, dc, :]):
                                mm = pe.matmul(hid[:, j, hc, :], a, b, start=(k == 0), stop=(k == 3 * DC - 1))
                                k += 1
                mm.then_inc(hid_done, 1)

            def down(n, slot, first, last):
                pe.wait_ge(g_hi, n + 1)
                pe.wait_ge(g_lo, n + 1)
                for t in range(RT):
                    k = 0
                    for hc in range(HH):
                        for a, b in split_passes(lambda i: gs[:, slot, i, hc, t * P:(t + 1) * P],
                                                 lambda i: ws[:, slot, i, 2, hc * D:(hc + 1) * D]):
                            mm = pe.matmul(yb[:, t, :], a, b, start=(first and k == 0), stop=(last and k == 5),
                                           skip_group_check=True)
                            k += 1
                mm.then_inc(y_done, 1)

            pe.wait_ge(x_hi, 1)
            pe.wait_ge(x_lo, 1)
            pe.wait_ge(spread_out, NE)
            hidden(0, 0)
            hidden(1, 1)
            down(0, 0, True, False)
            with pe.Fori(0, NE // 2) as i:
                for u in range(2):
                    n = NS + 2 * i + u
                    hidden(n, u)
                    down(n - 1, (u + 1) % 2, False, False)
            down(NS + NE - 1, 1, False, True)


class Named:
    pass


def perceiver_kernel(nc, x, ctx_1024, Wq, Wk, Wv, gru_wih, gru_whh, gru_bih, gru_bhh, slot_norm_w, input_norm_w,
                     Wqkv, bqkv, Wo, bo, router_w, router_b, routed_w1, routed_w3, routed_w2,
                     shared_w1, shared_w3, shared_w2, out):
    dram = Named()
    dram.x, dram.ctx, dram.Wq, dram.Wk, dram.Wv = x, ctx_1024, Wq, Wk, Wv
    dram.gru_wih, dram.gru_whh, dram.gru_bih, dram.gru_bhh = gru_wih, gru_whh, gru_bih, gru_bhh
    dram.slot_norm_w, dram.input_norm_w = slot_norm_w, input_norm_w
    dram.Wqkv, dram.bqkv, dram.Wo, dram.bo = Wqkv, bqkv, Wo, bo
    dram.router_w, dram.router_b = router_w, router_b
    dram.routed, dram.shared = (routed_w1, routed_w3, routed_w2), (shared_w1, shared_w3, shared_w2)
    h0_dram = nc.dram_tensor("h0_dram", [PAIRS, P, DC * P], F32).ap()
    h_dram = nc.dram_tensor("h_dram", [PAIRS, P, DC * P], F32).ap()
    with ExitStack() as ctx:
        def sb(name, shape, dt):
            return ctx.enter_context(nc.sbuf_tensor(name, shape, dt))

        c = Named()
        c.ident32, c.ident16 = sb("ident32", [P, P], F32), sb("ident16", [P, P], F16)
        c.ones32, c.ones16 = sb("ones32", [P, P], F32), sb("ones16", [P, P], F16)
        c.b_rz, c.b_n = sb("b_rz", [P, 2 * DC], F32), sb("b_n", [P, 2 * DC], F32)
        with ExitStack() as inner:
            w = Named()
            w.A = inner.enter_context(nc.sbuf_tensor("A", [P, 2, DC, D], F16))
            w.Bt = inner.enter_context(nc.sbuf_tensor("Bt", [P, 2, DC, G3], F16))
            w.whhT = inner.enter_context(nc.sbuf_tensor("whhT", [P, 2, DC, G3], F16))
            prepare_weights(nc, w, c, dram, h0_dram)
            slot_attention(nc, w, c, dram, h0_dram, h_dram)
        rows = ctx.enter_context(nc.sbuf_tensor("rows", [P, RT, D], F32))
        with ExitStack() as inner:
            folded = [inner.enter_context(nc.sbuf_tensor(name, [HD, HC, ROWS], F32)) for name in ("qT", "kT", "vT")]
            project_qkv(nc, c, dram, h_dram, rows, folded)
            head_attention(nc, c, dram, rows, folded)
        experts(nc, c, dram, rows, out)


_INS = ['x', 'ctx_1024', 'L0_xattn_Wq', 'L0_xattn_Wk', 'L0_xattn_Wv', 'L0_xattn_gru_wih', 'L0_xattn_gru_whh',
        'L0_xattn_gru_bih', 'L0_xattn_gru_bhh', 'L0_xattn_slot_norm_w', 'L0_xattn_input_norm_w', 'L0_attn_Wqkv',
        'L0_attn_bqkv', 'L0_attn_Wo', 'L0_attn_bo', 'L0_ffn_router_w', 'L0_ffn_router_b', 'L0_ffn_routed_w1',
        'L0_ffn_routed_w3', 'L0_ffn_routed_w2', 'L0_ffn_shared_w1', 'L0_ffn_shared_w3', 'L0_ffn_shared_w2']
_OUTS = [((8, 64, 512), 'float32')]


def kernel(**inputs):
    import numpy as _np
    import concourse.bacc as _bacc
    from concourse import mybir as _mybir
    from concourse.bass_utils import run_bass_kernel_spmd as _run

    nc = _bacc.Bacc("TRN2", target_bir_lowering=False, num_devices=1)
    arrays, args = {}, []
    for name in _INS:
        a = _np.ascontiguousarray(inputs[name])
        arrays[f"in_{name}_dram"] = a
        args.append(nc.dram_tensor(f"in_{name}_dram", a.shape, _mybir.dt.from_np(a.dtype), kind="ExternalInput").ap())
    for i, (shape, dtype) in enumerate(_OUTS):
        dt = _mybir.dt.from_np(_np.dtype(dtype))
        args.append(nc.dram_tensor(f"out_{i}_dram", shape, dt, kind="ExternalOutput").ap())
    perceiver_kernel(nc, *args)
    r = _run(nc, [arrays], core_ids=[0])
    got = tuple(r.results[0][f"out_{i}_dram"] for i in range(len(_OUTS)))
    return got[0]
```

```python
from contextlib import ExitStack

import concourse.bass as bass
from concourse import mybir

F32 = mybir.dt.float32
F16 = mybir.dt.float16
I32 = mybir.dt.int32
ALU = mybir.AluOpType
ACT = mybir.ActivationFunctionType
AX = mybir.AxisListType.X

P = 128
B, K, D, M = 8, 64, 512, 1601
DC = D // P
MT = -(-M // P)
TAIL = M - (MT - 1) * P
GROUPS = ((0, 8), (8, MT))
assert MT - 1 == 12
ITERS = 3
PAIRS = B // 2
G3 = 3 * D
GC = G3 // P
ROWS = B * K
RT = ROWS // P
WS = 128.0
AS = 32768.0
SLOT_SCALE = float(D) ** -0.5
RMS_EPS = 1e-6
LN_EPS = 1e-5
HC = 16
HD = D // HC
HG = HC // 4
NJ = 3 * HG
GB = 8
HEAD_SCALE = float(HD) ** -0.5
NE, NS = 8, 2
HH = 2
GS = 4.0
MAGIC = 1597463007.0


class Steps:

    def __init__(self, eng, sem):
        self.eng, self.sem, self.base, self.n = eng, sem, 0, 0

    def __call__(self, ins):
        self.n += 1
        ins.then_inc(self.sem, 1)
        return self.n

    def after(self, n):
        self.eng.wait_ge(self.sem, self.base + n)


def rsqrt(dve, st, v, y, t):
    st.after(st(dve.tensor_scalar(y.bitcast(I32), v.bitcast(I32), -0.5, MAGIC, ALU.mult, ALU.add)))
    for _ in range(3):
        st.after(st(dve.tensor_tensor(t, y, y, ALU.mult)))
        st.after(st(dve.scalar_tensor_tensor(t, t, -0.5, v, ALU.mult, ALU.mult)))
        st.after(st(dve.scalar_tensor_tensor(y, t, 1.5, y, ALU.add, ALU.mult)))


def layernorm(dve, st, src, dst, stats, mv, small, ready):
    for t in range(RT):
        n = st(dve.bn_stats(stats[:, t], src[:, t]))
    st.after(n)
    for t in range(RT):
        n = st(dve.bn_aggr(mv[:, t], stats[:, t]))
    st.after(n)
    normalise(dve, st, src, dst, mv, small, ready)


def normalise(dve, st, src, dst, mv, small, ready):
    var, rstd, tmp = (small[:, j] for j in range(3))
    st.after(st(dve.tensor_scalar(var, mv[:, :, 1], LN_EPS, None, ALU.add)))
    rsqrt(dve, st, var, rstd, tmp)
    for t in range(RT):
        dve.tensor_scalar(dst[:, t], src[:, t], mv[:, t, 0:1], rstd[:, t:t + 1], ALU.subtract,
                          ALU.mult).then_inc(ready, 1)


def split_passes(lhs, rhs):
    return [(lhs(0), rhs(0)), (lhs(0), rhs(1)), (lhs(1), rhs(0))]


def words(buf):
    return buf[:].rearrange("p t s c m -> p (t s c m)").bitcast(F32)


def load_context(sp, dram, big, pair, n, groups=(0, 1)):
    rows = dram.ctx[bass.ds(pair * 2 + n, 1)].rearrange("a m d -> (a m) d")
    for j in [j for j in range((MT - 1) // 4) if j // 2 in groups]:
        dst = words(big.ctxT[n])[:, 4 * j * D:4 * (j + 1) * D]
        src = rows[4 * P * j:4 * P * (j + 1), :].rearrange("(p t) d -> p (t d)", t=4)
        sp.dma_start(dst, src).then_inc(big.ctx_in[j // 2][n], 16)
    if 1 in groups:
        sp.dma_start(big.tail[n][0:TAIL, :], rows[(MT - 1) * P:M, :]).then_inc(big.ctx_in[1][n], 16)


def raw_tile(big, n, t):
    return big.tail[n][:] if t == MT - 1 else words(big.ctxT[n])[:, t * D:(t + 1) * D]


def square(act, big, dropped, pair, n, t):
    for g, (start, _) in enumerate(GROUPS):
        if t == start:
            act.wait_ge(big.ctx_in[g][n], (pair + 1) * 32)
    act.activation(dropped, raw_tile(big, n, t), ACT.Square, accum_out=big.ssq[n][:, t:t + 1]).then_inc(big.squares[n], 1)


def prepare_weights(nc, w, c, dram, slots, xr, big):
    sems = []
    with ExitStack() as ctx:
        def sb(name, shape, dt=F32):
            return ctx.enter_context(nc.sbuf_tensor(name, shape, dt))

        def sem(name):
            sems.append(nc.alloc_semaphore(name=name))
            return sems[-1]

        bank = ctx.enter_context(nc.psum_tensor("w_bank", [P, 8, 512], F32))
        stats = sb("stats", [P, RT, 6])
        mv = sb("mv", [P, RT, 2])
        small = sb("ln_small", [P, 3, RT])
        wqkv_raw = sb("wqkv_raw", [P, 3, DC, D])
        wqkv_s = sb("wqkv_s", [P, 3, 2, DC, D], F16)
        wih_raw = words(big.ctxT[1])[:, 0:GC * D].rearrange("p (c d) -> p c d", c=GC)
        wihT = sb("wihT", [P, 2, DC, G3], F16)
        whh_raw = wqkv_raw[:].rearrange("p j c d -> p (j c) d")
        w_in_row = words(big.ctxT[1])[:, GC * D:(GC + 1) * D]
        vec_rows = sb("vec_rows", [2 * DC + 2 * GC, P])
        vecs = sb("vecs", [P, 2 * DC + 2 * GC])
        w_slot, w_in = vecs[:, 0:DC], vecs[:, DC:2 * DC]
        bih, bhh = vecs[:, 2 * DC:2 * DC + GC], vecs[:, 2 * DC + GC:]
        f32row = sb("f32row", [P, 2, D])

        wih_in = [sem(f"wih_in{g}") for g in range(3)]
        x_in, small_in, wqk_in, wv_in, whh_in = (sem(n) for n in (
            "x_in", "small_in", "wqk_in", "wv_in", "whh_in"))
        consts_done = sem("w_consts_done")
        tail_zero = sem("tail_zero")
        vecs_turned = sem("vecs_turned")
        vecs_out = sem("vecs_out")
        dve_done = sem("w_dve_done")
        xn_ready = sem("xn_ready")
        xT_done = sem("xT_done")
        h0_ready = sem("h0_ready")
        qkv_hi = sem("qkv_hi")
        qkv_split = sem("qkv_split")
        turned = sem("turned")
        turned_hi = sem("turned_hi")
        turned_lo = sem("turned_lo")
        folded = sem("folded")
        folded_f32 = sem("folded_f32")
        folded_hi = sem("folded_hi")
        folded_lo = sem("folded_lo")

        NF = DC + DC * 3
        order = [("fold", 0), ("fold", 1), ("turn", 0), ("turn", 1), ("fold", 2), ("turn", 2), ("turn", 3), ("fold", 3)]
        for f in range(DC, NF):
            order += [("fold", f)] + [("turn", t) for t in range(2 * f - DC, 2 * f - DC + 2) if t < 2 * GC]
        TURN_X = 2 * DC
        turned_view = lambda t: bank[:, 4 + t % 4, :].rearrange("p (c g) -> p c g", c=DC)

        def turn_dst(t, part):
            dst = wihT if t < GC else w.whhT
            g = t % GC
            return dst[:, part, :, g * P:(g + 1) * P]

        def fold_dst(f, part):
            if f < DC:
                return w.A[:, part, f, :]
            g, dc = divmod(f - DC, DC)
            return w.Bt[:, part, dc, g * D:(g + 1) * D]

        block = ctx.enter_context(nc.Block())

        @block.sync
        def _(sp):
            sp.dma_start(wqkv_raw[:, 0], dram.Wq.rearrange("(c p) d -> p c d", p=P)).then_inc(wqk_in, 16)
            sp.dma_start(wqkv_raw[:, 1], dram.Wk.rearrange("(c p) d -> p c d", p=P)).then_inc(wqk_in, 16)
            sp.dma_start(w_in_row, dram.input_norm_w.partition_broadcast(P)).then_inc(small_in, 16)
            at = 0
            for src in (dram.slot_norm_w, dram.input_norm_w, dram.gru_bih, dram.gru_bhh):
                rows = src.shape[0] // P
                sp.dma_start(vec_rows[at:at + rows, :], src.rearrange("(c p) -> c p", p=P)).then_inc(small_in, 16)
                at += rows
            sp.dma_start(xr[:], dram.x.rearrange("b k d -> (b k) d").rearrange("(t p) d -> p t d", p=P)).then_inc(x_in, 16)
            for g in range(3):
                sp.dma_start(wih_raw[:, DC * g:DC * (g + 1)], dram.gru_wih[g * D:(g + 1) * D, :]
                             .rearrange("(c p) d -> p c d", p=P)).then_inc(wih_in[g], 16)
                if g == 0:
                    sp.dma_start(wqkv_raw[:, 2], dram.Wv.rearrange("(c p) d -> p c d", p=P)).then_inc(wv_in, 16)
            sp.wait_ge(tail_zero, 2)
            load_context(sp, dram, big, 0, 0, (0,))
            sp.wait_ge(qkv_split, 3)
            sp.dma_start(whh_raw, dram.gru_whh.rearrange("(c p) d -> p c d", p=P)).then_inc(whh_in, 16)
            load_context(sp, dram, big, 0, 0, (1,))
            sp.wait_ge(turned, GC)
            load_context(sp, dram, big, 0, 1)

        @block.gpsimd
        def _(pool):
            for n in range(2):
                pool.memset(big.tail[n][:], 0.0).then_inc(tail_zero, 1)
            pool.memset(c.ident32[:], 0.0).then_inc(consts_done, 1)
            pool.memset(c.ones32[:], 1.0).then_inc(consts_done, 1)
            pool.wait_ge(consts_done, 2)
            pool.affine_select(out=c.ident32[:], in_=c.ident32[:], compare_op=ALU.not_equal, fill=1.0,
                               base=0, pattern=[[-1, P]], channel_multiplier=1).then_inc(consts_done, 1)
            pool.wait_ge(consts_done, 3)
            pool.tensor_copy(c.ident16[:], c.ident32[:]).then_inc(consts_done, 1)

        @block.scalar
        def _(act):

            def raw_high(j):
                act.activation(wqkv_s[:, j, 0], wqkv_raw[:, j], ACT.Copy, scale=WS).then_inc(qkv_hi, 1)

            act.wait_ge(wqk_in, 32)
            raw_high(0)
            raw_high(1)
            def turned_block(t):
                act.wait_ge(turned, t + 1)
                act.activation(turn_dst(t, 0), turned_view(t), ACT.Copy, scale=WS).then_inc(turned_hi, 1)

            def folded_row(f):
                act.wait_ge(folded_f32, f + 1)
                act.copy(fold_dst(f, 0), f32row[:, f % 2]).then_inc(folded_hi, 1)

            for kind, k in order:
                if kind == "fold":
                    folded_row(k)
                    if k == TURN_X:
                        for t in range(RT):
                            act.wait_ge(xT_done, t + 1)
                            act.copy(slots[:, t].rearrange("p c r -> p (c r)"), bank[:, 2 + t % 2, :]).then_inc(h0_ready, 1)
                else:
                    turned_block(k)
                    if k == 1:
                        act.wait_ge(wv_in, 16)
                        raw_high(2)
                    if k >= GC:
                        if k > GC:
                            act.wait_ge(big.squares[0], k - GC)
                        square(act, big, w_in_row, 0, 0, k - GC)
            act.wait_ge(big.squares[0], MT - 1)
            square(act, big, w_in_row, 0, 0, MT - 1)

        @block.vector
        def _(dve):
            st = Steps(dve, dve_done)

            def split_raw(j):
                src = wqkv_raw[:, j].rearrange("p c d -> p (c d)")
                hi, lo = (wqkv_s[:, j, n].rearrange("p c d -> p (c d)") for n in range(2))
                dve.wait_ge(qkv_hi, j + 1)
                dve.scalar_tensor_tensor(lo, src, WS, hi, ALU.mult, ALU.subtract).then_inc(qkv_split, 1)

            def turned_block(t):
                dve.wait_ge(turned_hi, t + 1)
                dve.scalar_tensor_tensor(turn_dst(t, 1), turned_view(t), WS, turn_dst(t, 0), ALU.mult,
                                         ALU.subtract).then_inc(turned_lo, 1)

            def folded_row(f):
                dve.wait_ge(folded, f + 1)
                if f >= 2:
                    dve.wait_ge(folded_hi, f - 1)
                if f < DC:
                    dve.scalar_tensor_tensor(f32row[:, f % 2], bank[:, f % 2, :], w_slot[:, f:f + 1], w_in_row,
                                             ALU.mult, ALU.mult).then_inc(folded_f32, 1)
                else:
                    dc = (f - DC) % DC
                    dve.tensor_scalar(f32row[:, f % 2], bank[:, f % 2, :], w_in[:, dc:dc + 1], None,
                                      ALU.mult).then_inc(folded_f32, 1)

            def folded_low(f):
                dve.wait_ge(folded_hi, f + 1)
                dve.tensor_tensor(fold_dst(f, 1), f32row[:, f % 2], fold_dst(f, 0), ALU.subtract).then_inc(folded_lo, 1)

            split_raw(0)
            split_raw(1)
            dve.wait_ge(small_in, 80)
            dve.wait_ge(vecs_turned, 1)
            dve.tensor_copy(vecs[:], bank[:, 7, 0:2 * DC + 2 * GC]).then_inc(vecs_out, 1)
            dve.wait_ge(vecs_out, 1)
            st(dve.tensor_scalar(vecs[:, 0:2 * DC], vecs[:, 0:2 * DC], 1.0 / WS, None, ALU.mult))
            st(dve.tensor_tensor(c.b_rz[:], bih[:, 0:8], bhh[:, 0:8], ALU.add))
            st(dve.tensor_copy(c.b_n[:, 0:DC], bhh[:, 8:12]))
            st.after(st(dve.tensor_copy(c.b_n[:, DC:8], bih[:, 8:12])))
            for kind, k in order:
                if kind == "fold":
                    folded_row(k)
                    folded_low(k)
                    if k == DC - 1:
                        dve.wait_ge(x_in, 16)
                        layernorm(dve, st, xr, xr, stats, mv, small, xn_ready)
                else:
                    turned_block(k)
                    if k == 1:
                        split_raw(2)

        @block.tensor
        def _(pe):
            pe.wait_ge(consts_done, 4)
            def turn(t, raw):
                if t >= 4:
                    pe.wait_ge(turned_lo, t - 3)
                for dc in range(DC):
                    mm = pe.transpose(bank[:, 4 + t % 4, dc * P:(dc + 1) * P], raw[:, t % GC, dc * P:(dc + 1) * P],
                                      c.ident32[:])
                mm.then_inc(turned, 1)

            def fold(f, lhs, rhs):
                if f >= 2:
                    pe.wait_ge(folded_f32, f - 1)
                n = 0
                for ec in range(DC):
                    for a, b in split_passes(lambda i: lhs(i, ec), lambda i: rhs(i, ec)):
                        mm = pe.matmul(bank[:, f % 2, :], a, b, start=(n == 0), stop=(n == 3 * DC - 1))
                        n += 1
                mm.then_inc(folded, 1)

            pe.wait_ge(qkv_split, 2)
            for kind, k in order:
                if kind == "fold" and k < DC:
                    fold(k, lambda i, ec: wqkv_s[:, 0, i, ec, k * P:(k + 1) * P], lambda i, ec: wqkv_s[:, 1, i, ec, :])
                    if k == 0:
                        pe.wait_ge(small_in, 80)
                        pe.transpose(bank[:, 7, 0:2 * DC + 2 * GC], vec_rows[:], c.ident32[0:2 * DC + 2 * GC, 0:2 * DC + 2 * GC])\
                            .then_inc(vecs_turned, 1)
                elif kind == "fold":
                    g, dc = divmod(k - DC, DC)
                    pe.wait_ge(qkv_split, 3)
                    pe.wait_ge(turned_lo, DC * (g + 1))
                    fold(k, lambda i, ec: wqkv_s[:, 2, i, ec, dc * P:(dc + 1) * P],
                         lambda i, ec: wihT[:, i, ec, g * D:(g + 1) * D])
                    if k == TURN_X:
                        for t in range(RT):
                            pe.wait_ge(xn_ready, t + 1)
                            if t >= 2:
                                pe.wait_ge(h0_ready, t - 1)
                            for dc in range(DC):
                                mm = pe.transpose(bank[:, 2 + t % 2, dc * P:(dc + 1) * P], xr[:, t, dc * P:(dc + 1) * P], c.ident32[:])
                            mm.then_inc(xT_done, 1)
                else:
                    if k == 0:
                        pe.wait_ge(vecs_out, 1)
                    if k < GC and k % DC == 0:
                        pe.wait_ge(wih_in[k // DC], 16)
                    if k == GC:
                        pe.wait_ge(whh_in, 16)
                    turn(k, wih_raw if k < GC else whh_raw)
    nc.clear_and_free_semaphores(sems)
    nc.all_engine_barrier()


def slot_attention(nc, w, c, dram, slots, rows, big, e):
    with ExitStack() as ctx:
        def sb(name, shape, dt=F32):
            return ctx.enter_context(nc.sbuf_tensor(name, shape, dt))

        def sem(name):
            return ctx.enter_context(nc.semaphore(name))

        def sems(name):
            return [sem(f"{name}{lane}") for lane in range(2)]

        ctxn = [sb(f"ctxn{n}", [P, MT, 2, D], F16) for n in range(2)]
        ctxT, tail, ctx_in = big.ctxT, big.tail, big.ctx_in
        ssq, squares = big.ssq, big.squares
        rrow = [sb(f"rrow{n}", [P, MT]) for n in range(2)]
        rtmp = [sb(f"rtmp{n}", [P, MT]) for n in range(2)]
        h = [sb(f"h{n}", [P, DC, K]) for n in range(2)]
        hs = [sb(f"hs{n}", [P, 2, DC, K], F16) for n in range(2)]
        qs = [sb(f"qs{n}", [P, 2, DC, K], F16) for n in range(2)]
        us = qs
        attn = [sb(f"attn{n}", [P, 2, MT, K], F16) for n in range(2)]
        scratch = [sb(f"scratch{n}", [P, 16 * K]) for n in range(2)]
        f32t = [sb(f"f32t{n}", [P, DC, K]) for n in range(2)]
        cand = f32t
        small = [sb(f"small{n}", [P, 3, K]) for n in range(2)]
        rowmax = [sb(f"rowmax{n}", [P, MT]) for n in range(2)]
        rowsum = [sb(f"rowsum{n}", [P, MT]) for n in range(2)]
        attn_sum = [sb(f"attn_sum{n}", [P, K]) for n in range(2)]

        score = [ctx.enter_context(nc.psum_tensor(f"score{n}", [P, 1024], F32)) for n in range(2)]
        gate = [ctx.enter_context(nc.psum_tensor(f"gate{n}", [P, 2, 512], F32)) for n in range(2)]

        def raw(n, t):
            return raw_tile(big, n, t)

        e32 = [s[:, 0:MT * K].rearrange("p (t k) -> p t k", k=K) for s in scratch]
        rz = [s[:, 0:512] for s in scratch]
        hn_xn = [s[:, 512:1024] for s in scratch]

        tile_high = sem("tile_high")
        normed = sem("normed")
        tile_split = sems("tile_split")
        tile_turned = sems("tile_turned")
        turned_out = sems("turned_out")
        h_first = sems("h_first")
        h_hi = sems("h_hi")
        h_sq = sems("h_sq")
        h_lo = sems("h_lo")
        q_done = sems("q_done")
        q_split = sems("q_split")
        scored = sems("scored")
        shifted = sems("shifted")
        expd = sems("expd")
        attn_f32 = sems("attn_f32")
        attn_hi = sems("attn_hi")
        attn_lo = sems("attn_lo")
        attn_summed = sems("attn_summed")
        updated = sems("updated")
        u_split = sems("u_split")
        gated = sems("gated")
        gates_f32 = sems("gates_f32")
        rz_tanh = sems("rz_tanh")
        cand_sum = sems("cand_sum")
        cand_tanh = sems("cand_tanh")
        h_new = sems("h_new")
        dve_done = sem("s_dve_done")

        block = ctx.enter_context(nc.Block())
        PAIR_OWN = 3 * STEP_OWN + 3 * 11 + MT

        def whole(pair, n):
            return slots[:, bass.ds(pair, 1), :, n * K:(n + 1) * K].rearrange("p a c k -> p (a c) k")

        def all_pairs(eng, body):
            with eng.Fori(0, PAIRS - 1) as pair:
                body(pair, True)
            body(PAIRS - 1, False)

        @block.sync
        def _(sp):
            with sp.Fori(1, PAIRS) as pair:
                for n in range(2):
                    sp.wait_ge(scored[n], pair * ITERS)
                    load_context(sp, dram, big, pair, n)
            sp.dma_start(rows[:], dram.x.rearrange("b k d -> (b k) d").rearrange("(t p) d -> p t d", p=P)).then_inc(big.x_in, 16)
            sp.wait_ge(scored[0], PAIRS * ITERS)
            load_wqkv(sp, dram, big)
            sp.wait_ge(scored[1], PAIRS * ITERS)
            for n in range(NS):
                load_w13(sp, dram.shared, n, e, n)
                load_w2(sp, dram.shared, n, e, n)

        @block.scalar
        def _(act):
            def slots_out(n, src):
                act.copy(hs[n][:, 0], src).then_inc(h_hi[n], 1)
                act.activation(hn_xn[n][:, 0:DC * K].rearrange("p (c k) -> p c k", c=DC), src,
                               ACT.Square).then_inc(h_sq[n], 1)

            def first_slots(pair, n):
                slots_out(n, whole(pair, n))
                act.copy(h[n][:], whole(pair, n)).then_inc(h_first[n], 1)

            def squared(pair, n, t):
                square(act, big, ctxn[n][:, t].rearrange("p s d -> p (s d)").bitcast(F32), pair, n, t)

            def high_tile(pair, t):
                act.activation(ctxn[1][:, t, 0], raw(1, t), ACT.Copy, scale=rrow[1][:, t:t + 1]).then_inc(tile_high, 1)

            def tile_out(pair, n, t):
                act.wait_ge(tile_turned[n], pair * MT + t + 1)
                act.copy(ctxT[n][:, t].rearrange("p s c m -> p (s c m)").bitcast(F32),
                         score[n][:, t % 2 * 512:t % 2 * 512 + 512]).then_inc(turned_out[n], 1)

            def exponentials(n, step):
                act.wait_ge(shifted[n], step)
                act.activation(e32[n], e32[n], ACT.Exp, scale=SLOT_SCALE).then_inc(expd[n], 1)

            def attn_high(n, step):
                act.wait_ge(attn_f32[n], step)
                act.copy(attn[n][:, 0], e32[n]).then_inc(attn_hi[n], 1)

            TURNED = 5

            def lane_1_squares(pair, done):
                each = 2 if done else 1
                for t in range(MT - done):
                    tile_out(pair, 0, done + t)
                    for u in range(min(each * t, MT), min(each * (t + 1), MT)):
                        squared(pair, 1, u)

            def pair_rounds(pair, has_next):
                act.wait_ge(normed, pair + 1)
                for t in range(MT):
                    high_tile(pair, t)
                for it in range(ITERS):
                    step = pair * ITERS + it + 1
                    if it == 0:
                        for t in range(0, 2):
                            tile_out(pair, 1, t)
                        exponentials(0, step)
                        for t in range(2, 10):
                            tile_out(pair, 1, t)
                        attn_high(0, step)
                        for t in range(10, MT):
                            tile_out(pair, 1, t)
                    else:
                        exponentials(0, step)
                        attn_high(0, step)
                    exponentials(1, step)
                    attn_high(1, step)
                    early = it == ITERS - 1 and has_next
                    if early:
                        act.wait_ge(updated[0], step)
                        for t in range(*GROUPS[0]):
                            squared(pair + 1, 0, t)
                    for n in range(2):
                        act.wait_ge(gates_f32[n], step)
                        act.activation(rz[n], rz[n], ACT.Tanh, scale=0.5).then_inc(rz_tanh[n], 1)
                        if early and n == 1:
                            tile_out(pair + 1, 0, 3)
                        act.wait_ge(cand_sum[n], step)
                        act.activation(cand[n][:], f32t[n][:], ACT.Tanh).then_inc(cand_tanh[n], 1)
                        if early and n == 1:
                            tile_out(pair + 1, 0, 4)
                        if it < ITERS - 1:
                            act.wait_ge(h_new[n], step)
                            slots_out(n, h[n][:])
                        elif has_next:
                            act.wait_ge(h_new[n], step)
                            first_slots(pair + 1, n)
                            if n == 0:
                                for t in range(*GROUPS[1]):
                                    squared(pair + 1, 0, t)
                                for t in range(3):
                                    tile_out(pair + 1, 0, t)
                if has_next:
                    lane_1_squares(pair + 1, TURNED)

            for n in range(2):
                first_slots(0, n)
            lane_1_squares(0, 0)
            all_pairs(act, pair_rounds)

        @block.vector
        def _(dve):
            st = Steps(dve, dve_done)

            def slots_low(n, event, src):
                dve.wait_ge(h_hi[n], event)
                dve.tensor_tensor(hs[n][:, 1], src, hs[n][:, 0], ALU.subtract).then_inc(h_lo[n], 1)

            def norms(pair, n, a, b):
                dve.wait_ge(squares[n], pair * MT + b)
                st.after(st(dve.tensor_scalar(ssq[n][:, a:b], ssq[n][:, a:b], 1.0 / D, RMS_EPS, ALU.mult, ALU.add)))
                rsqrt(dve, st, ssq[n][:, a:b], rrow[n][:, a:b], rtmp[n][:, a:b])

            def low_tiles(pair, a, b):
                for t in range(a, b):
                    dve.wait_ge(tile_high, pair * MT + t + 1)
                    dve.scalar_tensor_tensor(ctxn[1][:, t, 1], raw(1, t), rrow[1][:, t:t + 1], ctxn[1][:, t, 0],
                                             ALU.mult, ALU.subtract).then_inc(tile_split[1], 1)

            def split_tiles(n, a, b):
                high = {}
                for t in range(a, b + 1):
                    if t < b:
                        high[t] = st(dve.tensor_scalar(ctxn[n][:, t, 0], raw(n, t), rrow[n][:, t:t + 1], None, ALU.mult))
                    if t > a:
                        st.after(high[t - 1])
                        dve.scalar_tensor_tensor(ctxn[n][:, t - 1, 1], raw(n, t - 1), rrow[n][:, t - 1:t],
                                                 ctxn[n][:, t - 1, 0], ALU.mult, ALU.subtract).then_inc(tile_split[n], 1)

            def q_out(n, step):
                v, y, t = (small[n][:, j] for j in range(3))
                dve.wait_ge(q_done[n], step)
                st.after(st(dve.tensor_scalar(v, score[n][:, 768:832], WS * WS / D, RMS_EPS * WS * WS, ALU.mult, ALU.add)))
                rsqrt(dve, st, v, y, t)
                st.after(st(dve.tensor_tensor(f32t[n][:], score[n][:, 512:768].rearrange("p (c k) -> p c k", c=DC),
                                              y.unsqueeze(1).to_broadcast([P, DC, K]), ALU.mult)))
                st.after(st(dve.tensor_copy(qs[n][:, 0], f32t[n][:])))
                dve.tensor_tensor(qs[n][:, 1], f32t[n][:], qs[n][:, 0], ALU.subtract).then_inc(q_split[n], 1)

            def softmax_shift(n, step):
                s = score[n][:, 0:MT * K].rearrange("p (t k) -> p t k", k=K)
                dve.wait_ge(scored[n], step)
                st.after(st(dve.tensor_reduce(rowmax[n][:], s, AX, ALU.max)))
                dve.tensor_tensor(e32[n], s, rowmax[n][:].unsqueeze(2).to_broadcast([P, MT, K]),
                                  ALU.subtract).then_inc(shifted[n], 1)

            def softmax_norm(n, step):
                dve.wait_ge(expd[n], step)
                st.after(st(dve.tensor_reduce(rowsum[n][:], e32[n], AX, ALU.add)))
                st.after(st(dve.reciprocal(rowsum[n][:], rowsum[n][:])))
                dve.scalar_tensor_tensor(e32[n], e32[n], AS, rowsum[n][:].unsqueeze(2).to_broadcast([P, MT, K]),
                                         ALU.mult, ALU.mult).then_inc(attn_f32[n], 1)

            def softmax_low(n, step):
                dve.wait_ge(attn_hi[n], step)
                dve.tensor_tensor(attn[n][:, 1], e32[n], attn[n][:, 0], ALU.subtract).then_inc(attn_lo[n], 1)

            def attn_sums(n, step):
                s = attn_sum[n]
                st.after(st(dve.tensor_reduce(s[:], e32[n][:, 0:MT - 1].rearrange("p t k -> p k t"), AX, ALU.add)))
                dve.tensor_tensor(s[0:TAIL], s[0:TAIL], e32[n][0:TAIL, MT - 1], ALU.add).then_inc(attn_summed[n], 1)

            def update_out(n, step):
                r = small[n][:, 0]
                dve.wait_ge(updated[n], step)
                st.after(st(dve.tensor_scalar(r, score[n][:, 256:320], RMS_EPS * AS, None, ALU.add)))
                st.after(st(dve.reciprocal(r, r)))
                st.after(st(dve.tensor_tensor(f32t[n][:], score[n][:, 0:256].rearrange("p (c k) -> p c k", c=DC),
                                              r.unsqueeze(1).to_broadcast([P, DC, K]), ALU.mult)))
                st.after(st(dve.tensor_copy(us[n][:, 0], f32t[n][:])))
                dve.tensor_tensor(us[n][:, 1], f32t[n][:], us[n][:, 0], ALU.subtract).then_inc(u_split[n], 1)

            def gates_in(n, step):
                dve.wait_ge(gated[n], step)
                for part, dst, bias in ((0, rz[n], c.b_rz), (1, hn_xn[n], c.b_n)):
                    ins = dve.scalar_tensor_tensor(dst.rearrange("p (c k) -> p c k", k=K),
                                                   gate[n][:, part, :].rearrange("p (c k) -> p c k", k=K), 1.0 / WS,
                                                   bias[:].unsqueeze(2).to_broadcast([P, 2 * DC, K]), ALU.mult, ALU.add)
                ins.then_inc(gates_f32[n], 1)

            def candidate(n, step):
                f = f32t[n][:].rearrange("p c k -> p (c k)")
                dve.wait_ge(rz_tanh[n], step)
                st.after(st(dve.scalar_tensor_tensor(f, rz[n][:, 0:256], 1.0, hn_xn[n][:, 0:256], ALU.add, ALU.mult)))
                dve.scalar_tensor_tensor(f, f, 0.5, hn_xn[n][:, 256:512], ALU.mult, ALU.add).then_inc(cand_sum[n], 1)

            def new_slots(n, step, dst):
                diff, z = (rz[n][:, a:a + 256].rearrange("p (c k) -> p c k", c=DC) for a in (0, 256))
                dve.wait_ge(cand_tanh[n], step)
                st.after(st(dve.tensor_tensor(diff, h[n][:], cand[n][:], ALU.subtract)))
                st.after(st(dve.scalar_tensor_tensor(diff, z, 1.0, diff, ALU.add, ALU.mult)))
                dve.scalar_tensor_tensor(dst, diff, 0.5, cand[n][:], ALU.mult, ALU.add).then_inc(h_new[n], 1)

            def pair_rounds(pair, has_next):
                st.base, st.n = MT + 2 * 11 + pair * PAIR_OWN, 0
                for it in range(ITERS):
                    step = pair * ITERS + it + 1
                    if it == 0:
                        norms(pair, 1, 0, MT)
                        dve.nop().then_inc(normed, 1)
                        q_out(0, step)
                        low_tiles(pair, 0, 6)
                        softmax_shift(0, step)
                        low_tiles(pair, 6, 9)
                        softmax_norm(0, step)
                        low_tiles(pair, 9, MT)
                        softmax_low(0, step)
                        q_out(1, step)
                    else:
                        softmax_shift(0, step)
                        q_out(1, step)
                        softmax_norm(0, step)
                        softmax_low(0, step)
                    softmax_shift(1, step)
                    attn_sums(0, step)
                    softmax_norm(1, step)
                    update_out(0, step)
                    softmax_low(1, step)
                    attn_sums(1, step)
                    gates_in(0, step)
                    if it < ITERS - 1:
                        candidate(0, step)
                        new_slots(0, step, h[0][:])
                        slots_low(0, step + 1, h[0][:])
                        update_out(1, step)
                        q_out(0, step + 1)
                        gates_in(1, step)
                        candidate(1, step)
                        new_slots(1, step, h[1][:])
                        slots_low(1, step + 1, h[1][:])
                    elif has_next:
                        norms(pair + 1, 0, *GROUPS[0])
                        candidate(0, step)
                        split_tiles(0, 0, 1)
                        update_out(1, step)
                        new_slots(0, step, whole(pair, 0))
                        split_tiles(0, 1, 2)
                        slots_low(0, step + 1, whole(pair + 1, 0))
                        split_tiles(0, 2, 4)
                        gates_in(1, step)
                        split_tiles(0, 4, 5)
                        candidate(1, step)
                        split_tiles(0, 5, 6)
                        new_slots(1, step, whole(pair, 1))
                        split_tiles(0, 6, 7)
                        slots_low(1, step + 1, whole(pair + 1, 1))
                        split_tiles(0, 7, 8)
                    else:
                        candidate(0, step)
                        new_slots(0, step, whole(pair, 0))
                        update_out(1, step)
                        gates_in(1, step)
                        candidate(1, step)
                        new_slots(1, step, whole(pair, 1))
                if has_next:
                    norms(pair + 1, 0, *GROUPS[1])
                    split_tiles(0, *GROUPS[1])
                    assert st.n == PAIR_OWN, (st.n, PAIR_OWN)

            for g, (a, b) in enumerate(GROUPS):
                norms(0, 0, a, b)
                split_tiles(0, a, b)
                slots_low(g, 1, whole(0, g))
            assert st.n == MT + 2 * 11, st.n
            all_pairs(dve, pair_rounds)

        @block.tensor
        def _(pe):
            def turn(pair, n):
                for t in range(MT):
                    pe.wait_ge(tile_split[n], pair * MT + t + 1)
                    if t >= 2:
                        pe.wait_ge(turned_out[n], pair * MT + t - 1)
                    dst = score[n][:, t % 2 * 512:t % 2 * 512 + 512].bitcast(F16)
                    for j in range(2 * DC):
                        s, dc = divmod(j, DC)
                        mm = pe.transpose(dst[:, j * P:(j + 1) * P], ctxn[n][:, t, s, dc * P:(dc + 1) * P], c.ident16[:])
                    mm.then_inc(tile_turned[n], 1)

            def chunks(dst, weights, operand, start):
                for o in range(len(dst)):
                    for dc in range(DC):
                        for a, b in split_passes(lambda i: weights(i, dc, o), lambda i: operand[:, i, dc]):
                            mm = pe.matmul(dst[o], a, b, start=start, stop=True, skip_group_check=True)
                            start = False
                return mm

            def query(pair, step, n):
                pe.wait_ge(turned_out[n], (pair + 1) * MT)
                pe.wait_ge(h_sq[n], step)
                for dc in range(DC):
                    pe.matmul(score[n][:, 768:832], c.ones32[:], hn_xn[n][:, dc * K:(dc + 1) * K], start=(dc == 0),
                              stop=True, skip_group_check=True)
                pe.wait_ge(h_hi[n], step)
                pe.wait_ge(h_lo[n], step)
                chunks([score[n][:, 512 + o * K:512 + (o + 1) * K] for o in range(DC)],
                       lambda i, dc, o: w.A[:, i, dc, o * P:(o + 1) * P], hs[n], False).then_inc(q_done[n], 1)

            def gate_cols(n, g):
                return gate[n][:, g // 8, g % 8 * K:(g % 8 + 1) * K]

            def hidden_rz(n):
                chunks([gate_cols(n, g) for g in range(8)], lambda i, dc, o: w.whhT[:, i, dc, o * P:(o + 1) * P],
                       hs[n], True)

            def hidden_n(n):
                chunks([gate_cols(n, 8 + g) for g in range(4)],
                       lambda i, dc, o: w.whhT[:, i, dc, (8 + o) * P:(9 + o) * P], hs[n], True)

            def scores(step, n):
                pe.wait_ge(q_split[n], step)
                for t in range(MT):
                    k = 0
                    for dc in range(DC):
                        for a, b in split_passes(lambda i: ctxT[n][:, t, i, dc], lambda i: qs[n][:, i, dc]):
                            mm = pe.matmul(score[n][:, t * K:(t + 1) * K], a, b, start=(k == 0), stop=(k == 3 * DC - 1),
                                           skip_group_check=True)
                            k += 1
                mm.then_inc(scored[n], 1)

            def update(step, n):
                pe.wait_ge(attn_hi[n], step)
                pe.wait_ge(attn_lo[n], step)
                rows = [P] * (MT - 1) + [TAIL]
                first = True
                for dc in range(DC):
                    for t in range(MT):
                        for a, b in split_passes(lambda i: ctxn[n][0:rows[t], t, i, dc * P:(dc + 1) * P],
                                                 lambda i: attn[n][0:rows[t], i, t]):
                            mm = pe.matmul(score[n][:, dc * K:(dc + 1) * K], a, b, start=first, stop=True,
                                           skip_group_check=True)
                            first = False
                pe.wait_ge(attn_summed[n], step)
                mm = pe.matmul(score[n][:, 256:320], c.ones32[:], attn_sum[n][:], start=False, stop=True, skip_group_check=True)
                mm.then_inc(updated[n], 1)

            def inputs(step, n):
                pe.wait_ge(u_split[n], step)
                cols = [gate_cols(n, g) for g in range(8)] + [gate_cols(n, 12 + g) for g in range(4)]
                chunks(cols, lambda i, dc, o: w.Bt[:, i, dc, o * P:(o + 1) * P], us[n], False).then_inc(gated[n], 1)

            def pair_rounds(pair, has_next):
                for it in range(ITERS):
                    step = pair * ITERS + it + 1
                    if it == 0:
                        query(pair, step, 0)
                    hidden_rz(0)
                    scores(step, 0)
                    if it == 0:
                        turn(pair, 1)
                    query(pair, step, 1)
                    hidden_rz(1)
                    scores(step, 1)
                    update(step, 0)
                    hidden_n(0)
                    hidden_n(1)
                    inputs(step, 0)
                    update(step, 1)
                    if it < ITERS - 1:
                        query(pair, step + 1, 0)
                    inputs(step, 1)
                if has_next:
                    turn(pair + 1, 0)

            turn(0, 0)
            all_pairs(pe, pair_rounds)


STEP_OWN = 2 * (1 + (1 + 10 + 2) + 1 + 2 + 4 + 1 + 2)


def wqkv_rows(big):
    return words(big.ctxT[0])[:, 0:NJ * D].rearrange("p (j d) -> p j d", j=NJ)


def load_wqkv(sp, dram, big):
    w_rows = dram.Wqkv.rearrange("(i ii s e) d -> ii s e i d", i=HG, ii=4, s=3)
    for s in range(3):
        for ii in range(4):
            sp.dma_start(wqkv_rows(big)[32 * ii:32 * ii + 32, HG * s:HG * s + HG, :], w_rows[ii, s]).then_inc(big.wqkv_in, 16)


def project_qkv(nc, c, dram, slots, rows, folded, wT, woT, big):
    with ExitStack() as ctx:
        def sb(name, shape, dt=F32):
            return ctx.enter_context(nc.sbuf_tensor(name, shape, dt))

        def sem(name):
            return ctx.enter_context(nc.semaphore("p_" + name))

        bank = ctx.enter_context(nc.psum_tensor("p_bank", [P, 8, 512], F32))
        xn = slots[:].rearrange("p t c r -> p t (c r)")
        xT = sb("p_xT", [P, 2, DC, ROWS], F16)
        raw = wqkv_rows(big)
        wo_raw = sb("p_wo_raw", [P, DC, D])
        bias_rows = sb("p_bias_rows", [NJ, P])
        bias = sb("p_bias", [P, NJ])
        stats = sb("p_stats", [P, RT, 6])
        mv = sb("p_mv", [P, RT, 2])
        small = sb("p_small", [P, 3, RT])

        wo_in, b_in, h_rows, x_rows, xn_ready, x_turned, x_hi, x_lo, turned, turned_hi, turned_lo, \
            b_turned, b_out, projected, proj_out, moved, dve_done = (sem(n) for n in (
                "wo_in", "b_in", "h_rows", "x_rows", "xn_ready", "x_turned", "x_hi", "x_lo", "turned",
                "turned_hi", "turned_lo", "b_turned", "b_out", "projected", "proj_out", "moved", "dve_done"))

        def turned_dst(j, part):
            if j < NJ:
                return wT[:, part, :, j * P:(j + 1) * P]
            return woT[:, part, :, (j - NJ) * P:(j - NJ + 1) * P]

        b_rows = dram.bqkv.rearrange("(i ii s e) -> s i ii e", i=HG, ii=4, s=3)

        AHEAD = DC

        block = ctx.enter_context(nc.Block())

        @block.sync
        def _(sp):
            sp.dma_start(wo_raw[:], dram.Wo.rearrange("(c p) d -> p c d", p=P)).then_inc(wo_in, 16)
            for s in range(2):
                sp.wait_ge(proj_out, HG * (s + 1))
                for ii in range(4):
                    sp.dma_start(folded[s][:, ii:HC:4, :], raw[32 * ii:32 * ii + 32, HG * s:HG * s + HG, :]).then_inc(moved, 16)
            sp.wait_ge(moved, 8 * 16)

        @block.scalar
        def _(act):
            for s in range(3):
                act.dma_start(bias_rows[HG * s:HG * s + HG, :].rearrange("i (ii e) -> i ii e", ii=4),
                              b_rows[s]).then_inc(b_in, 16)
            def turned_high(j):
                act.wait_ge(turned, j + 1)
                act.activation(turned_dst(j, 0), bank[:, 4 + j % 4, :].rearrange("p (c g) -> p c g", c=DC),
                               ACT.Copy, scale=WS).then_inc(turned_hi, 1)

            for j in range(AHEAD):
                turned_high(j)
            for t in range(RT):
                act.wait_ge(x_turned, t + 1)
                act.copy(xT[:, 0, :, t * P:(t + 1) * P], bank[:, t, :].rearrange("p (c r) -> p c r", c=DC)).then_inc(x_hi, 1)
            act.wait_ge(b_out, 1)
            for j in range(NJ):
                turned_high(j + AHEAD)
                act.wait_ge(projected, j + 1)
                act.activation(raw[:, j, :], bank[:, j % 4, :], ACT.Identity, bias=bias[:, j:j + 1],
                               scale=1.0 / WS).then_inc(proj_out, 1)

        @block.vector
        def _(dve):
            st = Steps(dve, dve_done)
            dve.wait_ge(big.x_in, 16)
            for t in range(RT):
                dve.wait_ge(h_rows, t + 1)
                dve.tensor_tensor(rows[:, t], bank[:, t, :], rows[:, t], ALU.add).then_inc(x_rows, 1)
            dve.wait_ge(x_rows, RT)
            layernorm(dve, st, rows, xn, stats, mv, small, xn_ready)
            def turned_low(j):
                dve.wait_ge(turned_hi, j + 1)
                dve.scalar_tensor_tensor(turned_dst(j, 1), bank[:, 4 + j % 4, :].rearrange("p (c g) -> p c g", c=DC),
                                         WS, turned_dst(j, 0), ALU.mult, ALU.subtract).then_inc(turned_lo, 1)

            for j in range(AHEAD):
                turned_low(j)
            for t in range(RT):
                dve.wait_ge(x_hi, t + 1)
                dve.tensor_tensor(xT[:, 1, :, t * P:(t + 1) * P], bank[:, t, :].rearrange("p (c r) -> p c r", c=DC),
                                  xT[:, 0, :, t * P:(t + 1) * P], ALU.subtract).then_inc(x_lo, 1)
            dve.wait_ge(b_turned, 1)
            dve.tensor_copy(bias[:], bank[:, 0, 0:NJ]).then_inc(b_out, 1)
            for j in range(AHEAD, NJ + DC):
                turned_low(j)

        @block.tensor
        def _(pe):
            for t in range(RT):
                for dc in range(DC):
                    mm = pe.transpose(bank[:, t, dc * P:(dc + 1) * P], slots[:, t, dc], c.ident32[:])
                mm.then_inc(h_rows, 1)
            pe.wait_ge(big.wqkv_in, 12 * 16)
            def turn(j):
                if j >= 4:
                    pe.wait_ge(turned_lo, j - 3)
                if j == NJ:
                    pe.wait_ge(wo_in, 16)
                src = raw[:, j] if j < NJ else wo_raw[:, j - NJ]
                for dc in range(DC):
                    mm = pe.transpose(bank[:, 4 + j % 4, dc * P:(dc + 1) * P], src[:, dc * P:(dc + 1) * P], c.ident32[:])
                mm.then_inc(turned, 1)

            for j in range(AHEAD):
                turn(j)
            for t in range(RT):
                pe.wait_ge(xn_ready, t + 1)
                for dc in range(DC):
                    mm = pe.transpose(bank[:, t, dc * P:(dc + 1) * P], xn[:, t, dc * P:(dc + 1) * P], c.ident32[:])
                mm.then_inc(x_turned, 1)
            pe.wait_ge(x_lo, RT)
            pe.wait_ge(b_in, 48)
            pe.transpose(bank[:, 0, 0:NJ], bias_rows[:], c.ident32[0:NJ, 0:NJ]).then_inc(b_turned, 1)
            pe.wait_ge(b_out, 1)
            for j in range(NJ):
                turn(j + AHEAD)
                pe.wait_ge(turned_lo, j + 1)
                if j >= 4:
                    pe.wait_ge(proj_out, j - 3)
                n = 0
                for dc in range(DC):
                    for a, b in split_passes(lambda i: wT[:, i, dc, j * P:(j + 1) * P], lambda i: xT[:, i, dc, :]):
                        mm = pe.matmul(bank[:, j % 4, :], a, b, start=(n == 0), stop=(n == 3 * DC - 1))
                        n += 1
                mm.then_inc(projected, 1)


def head_attention(nc, c, dram, slots, rows, folded, woT, big, ex):
    qT, kT, vT = folded
    with ExitStack() as ctx:
        def sb(name, shape, dt=F32):
            return ctx.enter_context(nc.sbuf_tensor(name, shape, dt))

        def sem(name):
            return ctx.enter_context(nc.semaphore("t_" + name))

        score = ctx.enter_context(nc.psum_tensor("t_score", [P, 2, 512], F32))
        probT = ctx.enter_context(nc.psum_tensor("t_probT", [P, 2, 512], F32))
        value = ctx.enter_context(nc.psum_tensor("t_value", [P, 2, 512], F32))
        yb = ctx.enter_context(nc.psum_tensor("t_y", [P, 512], F32))
        vb = ctx.enter_context(nc.psum_tensor("t_vb", [P, 512], F32))
        q_heads = sb("t_q_heads", [HD, 2, 2 * GB, 64])
        v_heads = sb("t_v_heads", [HD, 2, GB, P])
        v = sb("t_v", [P, 2, GB, HD])
        e = sb("t_e", [P, 2, GB, 64])
        stat = sb("t_stat", [P, 2, 2, GB])
        third = 2 * GB * P
        prob, halves, pT = (words(big.ctxT[0])[:, i * third:(i + 1) * third] for i in range(3))
        prob, pT = (a.rearrange("p (s g q) -> p s g q", s=2, g=GB) for a in (prob, pT))
        valsS = halves.bitcast(F16).rearrange("p (s c t) -> p s c t", s=2, c=DC)
        vals = vT
        valsT = slots[:].rearrange("p t c r -> p (t c r)").rearrange("p (c t) -> p c t", c=DC)
        bo_row = sb("t_bo_row", [P, D])

        v_moved, bo_in, zeroed, q_ready, v_ready, v_turned, v_out, scored, shifted, expd, prob_out, prob_turned, pT_out, valued, vals_out, \
            vals_hi, vals_lo, y_done, y_out, bo_added, dve_done = (sem(n) for n in (
                "v_moved", "bo_in", "zeroed", "q_ready", "v_ready", "v_turned", "v_out", "scored", "shifted", "expd", "prob_out", "prob_turned",
                "pT_out", "valued", "vals_out", "vals_hi", "vals_lo", "y_done",
                "y_out", "bo_added", "dve_done"))

        moved = [sem(f"moved{t}") for t in range(RT)]

        block = ctx.enter_context(nc.Block())

        @block.sync
        def _(sp):
            for ii in range(4):
                sp.dma_start(vT[:, ii:HC:4, :], wqkv_rows(big)[32 * ii:32 * ii + 32, 2 * HG:3 * HG, :]).then_inc(v_moved, 16)
            sp.dma_start(bo_row[:], dram.bo.partition_broadcast(P)).then_inc(bo_in, 16)
            for t in range(RT):
                sp.wait_ge(vals_out, 4 * (t + 1))
                for ii in range(4):
                    sp.dma_start(valsT[32 * ii:32 * ii + 32, :, t * P:(t + 1) * P],
                                 vals[:, ii:HC:4, t * P:(t + 1) * P]).then_inc(moved[t], 16)

        @block.gpsimd
        def _(pool):
            pool.memset(prob, 0.0).then_inc(zeroed, 1)

        @block.scalar
        def _(act):
            def side_by_side(src, k):
                return src[:, :, 64 * k:64 * k + 64].rearrange("e c (m r) -> e m c r", r=4)

            def q_block(k):
                if k >= 2:
                    act.wait_ge(scored, k - 1)
                act.copy(q_heads[:, k % 2].rearrange("e m (c r) -> e m c r", r=4), side_by_side(qT, k)).then_inc(q_ready, 1)

            def v_block(k):
                if k >= 2:
                    act.wait_ge(v_turned, k - 1)
                act.copy(v_heads[:, k % 2].rearrange("e g (h c r) -> e (g h) c r", h=2, r=4),
                         side_by_side(vT, k)).then_inc(v_ready, 1)

            def v_in(k):
                act.wait_ge(v_turned, k + 1)
                if k >= 2:
                    act.wait_ge(valued, 2 * (k - 1))
                act.copy(v[:, k % 2].rearrange("p g e -> p (g e)"), vb[:, 0:GB * HD]).then_inc(v_out, 1)

            def probs_turned(k):
                for j in range(2):
                    act.wait_ge(prob_turned, 2 * k + j + 1)
                    if k >= 2:
                        act.wait_ge(valued, 2 * (k - 1))
                    act.copy(pT[:, k % 2, 4 * j:4 * j + 4, :].rearrange("p g q -> p (g q)"), probT[:, j, :]).then_inc(pT_out, 1)

            def vals_high(t):
                act.wait_ge(moved[t], 64)
                act.copy(valsS[:, 0, :, t * P:(t + 1) * P], valsT[:, :, t * P:(t + 1) * P]).then_inc(vals_hi, 1)

            def exponentials(k):
                act.wait_ge(shifted, k + 1)
                ek = e[:, k % 2].rearrange("p g k -> p (g k)")
                act.activation(ek, ek, ACT.Exp, scale=HEAD_SCALE).then_inc(expd, 1)

            for k in range(2):
                q_block(k)
            exponentials(0)
            act.wait_ge(v_moved, 64)
            for k in range(2):
                v_block(k)
            for k in range(B):
                if k + 2 < B:
                    q_block(k + 2)
                v_in(k)
                probs_turned(k)
                if k + 1 < B:
                    exponentials(k + 1)
                if k + 2 < B:
                    v_block(k + 2)
                if k >= 3 and k % 2 == 1:
                    vals_high((k - 3) // 2)
            vals_high(RT - 1)

        @block.vector
        def _(dve):
            st = Steps(dve, dve_done)
            def add_bo():
                dve.wait_ge(bo_in, 16)
                for t in range(RT):
                    dve.tensor_tensor(rows[:, t], rows[:, t], bo_row[:], ALU.add).then_inc(bo_added, 1)

            def shift(k):
                s = score[:, k % 2, :].rearrange("p (g k) -> p g k", k=64)
                dve.wait_ge(scored, k + 1)
                st.after(st(dve.tensor_reduce(stat[:, k % 2, 0], s, AX, ALU.max)))
                dve.tensor_tensor(e[:, k % 2], s, stat[:, k % 2, 0].unsqueeze(2).to_broadcast([P, GB, 64]),
                                  ALU.subtract).then_inc(shifted, 1)

            def norm(k):
                dve.wait_ge(expd, k + 1)
                total = stat[:, k % 2, 1]
                st.after(st(dve.tensor_reduce(total, e[:, k % 2], AX, ALU.add)))
                st.after(st(dve.reciprocal(total, total)))
                if k >= 2:
                    dve.wait_ge(prob_turned, 2 * (k - 1))
                if k == 0:
                    dve.wait_ge(zeroed, 1)
                for g in range(2):
                    half = slice(64 * g, 64 * g + 64)
                    ins = dve.tensor_tensor(prob[half, k % 2, :, half], e[half, k % 2],
                                            total[half].unsqueeze(2).to_broadcast([64, GB, 64]), ALU.mult)
                    ins.then_inc(prob_out, 1)

            def values_out(k):
                for j in range(2):
                    dve.wait_ge(valued, 2 * k + j + 1)
                    t0 = 64 * k + 32 * j
                    dst = vals[:, :, t0:t0 + 32].rearrange("e c (m r) -> e m c r", r=4)
                    dve.tensor_copy(dst, value[0:HD, j, :].rearrange("e (m c r) -> e m c r", c=HC, r=4)).then_inc(vals_out, 1)

            def vals_low(t):
                dve.wait_ge(vals_hi, t + 1)
                dve.tensor_tensor(valsS[:, 1, :, t * P:(t + 1) * P], valsT[:, :, t * P:(t + 1) * P],
                                  valsS[:, 0, :, t * P:(t + 1) * P], ALU.subtract).then_inc(vals_lo, 1)

            def add_y(t):
                dve.wait_ge(y_done, t + 1)
                dve.wait_ge(bo_added, RT)
                dve.scalar_tensor_tensor(rows[:, t], yb[:], 1.0 / WS, rows[:, t], ALU.mult, ALU.add).then_inc(y_out, 1)
                dve.wait_ge(y_out, t + 1)
                st.after(st(dve.bn_stats(ex.stats[:, t], rows[:, t])))
                st(dve.bn_aggr(ex.mv[:, t], ex.stats[:, t]))

            shift(0)
            for k in range(B):
                norm(k)
                if k + 1 < B:
                    shift(k + 1)
                if k == 1:
                    add_bo()
                if k >= 1:
                    values_out(k - 1)
                if k >= 3 and k % 2 == 1:
                    vals_low((k - 3) // 2)
                if k >= 5 and k % 2 == 1:
                    add_y((k - 5) // 2)
            values_out(B - 1)
            add_y(RT - 2)
            vals_low(RT - 1)
            add_y(RT - 1)

        @block.tensor
        def _(pe):
            def turn_v(k):
                pe.wait_ge(v_ready, k + 1)
                if k >= 1:
                    pe.wait_ge(v_out, k)
                for g in range(GB):
                    mm = pe.transpose(vb[:, g * HD:(g + 1) * HD], v_heads[:, k % 2, g, :], c.ident32[0:HD, 0:HD])
                mm.then_inc(v_turned, 1)

            def scores(k):
                pe.wait_ge(q_ready, k + 1)
                if k >= 2:
                    pe.wait_ge(shifted, k - 1)
                for g in range(GB):
                    for hd in range(2):
                        t0 = 64 * k + 8 * g + 4 * hd
                        mm = pe.matmul(score[64 * hd:64 * hd + 64, k % 2, g * 64:(g + 1) * 64], q_heads[:, k % 2, 2 * g + hd, :],
                                       kT[:, :, t0:t0 + 4], start=True, stop=True)
                mm.then_inc(scored, 1)

            def turn_probs(k):
                pe.wait_ge(prob_out, 2 * (k + 1))
                for j in range(2):
                    if k >= 1:
                        pe.wait_ge(pT_out, 2 * (k - 1) + j + 1)
                    for g in range(4):
                        mm = pe.transpose(probT[:, j, g * P:(g + 1) * P], prob[:, k % 2, 4 * j + g, :], c.ident32[:])
                    mm.then_inc(prob_turned, 1)

            def values(k):
                pe.wait_ge(v_out, k + 1)
                for j in range(2):
                    pe.wait_ge(pT_out, 2 * k + j + 1)
                    if k >= 1:
                        pe.wait_ge(vals_out, 2 * (k - 1) + j + 1)
                    for g in range(4):
                        mm = pe.matmul(value[0:HD, j, g * P:(g + 1) * P], v[:, k % 2, 4 * j + g, :],
                                       pT[:, k % 2, 4 * j + g, :], start=True, stop=True)
                    mm.then_inc(valued, 1)

            def project(t):
                pe.wait_ge(vals_lo, t + 1)
                if t >= 1:
                    pe.wait_ge(y_out, t)
                n = 0
                for dc in range(DC):
                    for a, b in split_passes(lambda i: valsS[:, i, dc, t * P:(t + 1) * P], lambda i: woT[:, i, dc, :]):
                        mm = pe.matmul(yb[:], a, b, start=(n == 0), stop=(n == 3 * DC - 1))
                        n += 1
                mm.then_inc(y_done, 1)

            scores(0)
            scores(1)
            for k in range(B):
                turn_v(k)
                turn_probs(k)
                if k + 2 < B:
                    scores(k + 2)
                if k >= 4 and k % 2 == 0:
                    project((k - 4) // 2)
                values(k)
            project(RT - 2)
            project(RT - 1)


def load_w13(eng, weights, ex, e, slot):
    for j in range(2):
        src = weights[j][bass.ds(ex, 1)].rearrange("a (c p) n -> (a p) c n", p=P)
        eng.dma_start(e.raw[:, slot, j].rearrange("p (c n) -> p c n", c=src.shape[1]), src).then_inc(e.w13_in[slot], 16)


def load_w2(eng, weights, ex, e, slot):
    src = weights[2][bass.ds(ex, 1)].rearrange("a (c p) n -> (a p) c n", p=P)
    eng.dma_start(e.raw[:, slot, 2].rearrange("p (c n) -> p c n", c=src.shape[1]), src).then_inc(e.w2_in[slot], 16)


def experts(nc, c, dram, rows, out, e):
    with ExitStack() as ctx:
        def sb(name, shape, dt=F32):
            return ctx.enter_context(nc.sbuf_tensor(name, shape, dt))

        def sem(name):
            return ctx.enter_context(nc.semaphore("e_" + name))

        yb = ctx.enter_context(nc.psum_tensor("e_y", [P, RT, D], F32))
        hid = ctx.enter_context(nc.psum_tensor("e_hid", [P, 2, HH, ROWS], F32))
        xn = sb("e_xn", [P, RT, D])
        xT = sb("e_xT", [P, DC, ROWS])
        xs = sb("e_xs", [P, 2, DC, ROWS], F16)
        small = sb("e_small", [P, 3, RT])
        rw = sb("e_rw", [P, DC, NE])
        rb_row = sb("e_rb_row", [P, NE])
        rank = sb("e_rank", [P, NE])
        lg = sb("e_lg", [P, RT, NE])
        key = sb("e_key", [P, RT, NE])
        pick1 = sb("e_pick1", [P, RT, NE])
        pick2 = sb("e_pick2", [P, RT, NE])
        rest = sb("e_rest", [P, RT, NE])
        col = sb("e_col", [P, 4, RT])
        gT = sb("e_gT", [NE, 2, ROWS], F16)
        sel = sb("e_sel", [NE, NE, P], F16)
        gate_row = sb("e_gate_row", [P, NE, ROWS])
        raw = e.raw
        ws = sb("e_ws", [P, 2, 2, 3, 1024], F16)
        th = sb("e_th", [P, HH * ROWS])
        gs = sb("e_gs", [P, 2, 2, HH, ROWS], F16)

        x_ready, x_turned, x_out, x_hi, x_lo, r_in, routed, gexp_in, gexp_out, gates_out, g_turned, gT_hi, gT_lo, \
            spread, spread_out, w13_hi, w13_lo, w2_hi, w2_lo, hid_done, tanhd, hid_read, g_f32, g_hi, g_lo, y_done, y_last, y_out, o_out, \
            consts, dve_done = (sem(n) for n in (
                "x_ready", "x_turned", "x_out", "x_hi", "x_lo", "r_in", "routed", "gexp_in", "gexp_out",
                "gates_out", "g_turned", "gT_hi", "gT_lo", "spread", "spread_out", "w13_hi", "w13_lo", "w2_hi", "w2_lo", "hid_done", "tanhd",
                "hid_read", "g_f32", "g_hi", "g_lo", "y_done", "y_last", "y_out", "o_out", "consts", "dve_done"))

        def experts_in_turn(eng, base, body):
            for n in range(NS):
                body(n, 0, n % 2, n, False)
            with eng.Fori(0, NE // 2 - 1) as i:
                base(i)
                for u in range(2):
                    body(NS + 2 * i + u, i + 1, u, 2 * i + u, True)
            base(NE // 2 - 1)
            for u in range(2):
                body(NS + NE - 2 + u, NE // 2, u, NE - 2 + u, True)

        def left(n, ahead):
            return not isinstance(n, int) or n + ahead < NS + NE

        block = ctx.enter_context(nc.Block())

        @block.sync
        def _(sp):
            sp.dma_start(rw[:], dram.router_w.rearrange("(c p) n -> p c n", p=P)).then_inc(r_in, 16)
            sp.dma_start(rb_row[:], dram.router_b.partition_broadcast(P)).then_inc(r_in, 16)

            with sp.Fori(0, NE // 2) as i:
                for u in range(2):
                    n = NS + 2 * i + u
                    sp.wait_ge(w13_lo, n - 1)
                    load_w13(sp, dram.routed, 2 * i + u, e, u)
                    sp.wait_ge(w2_lo, n - 1)
                    load_w2(sp, dram.routed, 2 * i + u, e, u)
            for t in range(RT):
                sp.wait_ge(y_out, t + 1)
                sp.dma_start(out.rearrange("b k d -> (b k) d")[t * P:(t + 1) * P, :], rows[:, t]).then_inc(o_out, 16)
            sp.wait_ge(o_out, 16 * RT)

        @block.gpsimd
        def _(pool):
            for n in range(NE):
                pool.memset(rank[:, n:n + 1], float(NE - n)).then_inc(consts, 1)

        @block.scalar
        def _(act):
            def high_w13(n, turn, slot):
                act.wait_ge(e.w13_in[slot], (turn + 1) * 32)
                if not isinstance(n, int) or n >= 2:
                    act.wait_ge(hid_done, n - 1)
                act.activation(ws[:, slot, 0, 0:2], raw[:, slot, 0:2], ACT.Copy, scale=WS).then_inc(w13_hi, 1)

            def high_w2(n, turn, slot):
                act.wait_ge(e.w2_in[slot], (turn + 1) * 16)
                if not isinstance(n, int) or n >= 2:
                    act.wait_ge(y_done, n - 1)
                act.activation(ws[:, slot, 0, 2], raw[:, slot, 2], ACT.Copy, scale=WS).then_inc(w2_hi, 1)

            high_w13(0, 0, 0)
            high_w2(0, 0, 0)
            for t in range(RT):
                act.wait_ge(x_turned, t + 1)
                act.copy(xT[:, :, t * P:(t + 1) * P], yb[:, t, :].rearrange("p (c r) -> p c r", c=DC)).then_inc(x_out, 1)
            act.wait_ge(x_out, RT)
            act.copy(xs[:, 0], xT[:]).then_inc(x_hi, 1)
            high_w13(1, 0, 1)
            act.wait_ge(gexp_in, 1)
            act.activation(lg[:], lg[:], ACT.Exp).then_inc(gexp_out, 1)
            def gates_spread(n):
                act.wait_ge(spread, n + 1)
                act.activation(gate_row[:, n], yb[:, (n + 2) % RT, :], ACT.Copy,
                               scale=0.5 / (WS * WS)).then_inc(spread_out, 1)

            def expert(n, turn, slot, ex, is_routed):
                act.wait_ge(hid_done, n + 1)
                if not isinstance(n, int) or n >= 1:
                    act.wait_ge(g_lo, n)
                act.activation(th[:], hid[:, 0].rearrange("p c t -> p (c t)"), ACT.Tanh, scale=0.5 / WS).then_inc(tanhd, 1)
                if isinstance(n, int) and n == 0:
                    act.wait_ge(g_turned, 1)
                    act.activation(gT[:, 0], yb[0:NE, 1, :], ACT.Copy, scale=GS).then_inc(gT_hi, 1)
                    for m in range(NE):
                        gates_spread(m)
                act.wait_ge(g_f32, n + 1)
                act.copy(gs[:, slot, 0], th[:].rearrange("p (c t) -> p c t", c=HH)).then_inc(g_hi, 1)
                if left(n, 1):
                    high_w2(n + 1, turn + slot, 1 - slot)
                if left(n, 2):
                    high_w13(n + 2, turn + 1, slot)

            experts_in_turn(act, lambda i: None, expert)

        @block.vector
        def _(dve):
            st = Steps(dve, dve_done)
            normalise(dve, st, rows, xn, e.mv, small, x_ready)

            def low_w13(n, slot):
                dve.wait_ge(w13_hi, n + 1)
                dve.scalar_tensor_tensor(ws[:, slot, 1, 0:2], raw[:, slot, 0:2], WS, ws[:, slot, 0, 0:2], ALU.mult,
                                         ALU.subtract).then_inc(w13_lo, 1)

            def low_w2(n, slot):
                dve.wait_ge(w2_hi, n + 1)
                dve.scalar_tensor_tensor(ws[:, slot, 1, 2], raw[:, slot, 2], WS, ws[:, slot, 0, 2], ALU.mult,
                                         ALU.subtract).then_inc(w2_lo, 1)

            low_w13(0, 0)
            dve.wait_ge(x_hi, 1)
            dve.tensor_tensor(xs[:, 1], xT[:], xs[:, 0], ALU.subtract).then_inc(x_lo, 1)
            st(dve.tensor_copy(sel[:], c.ident32[0:NE, 0:NE].unsqueeze(2).to_broadcast([NE, NE, P])))
            dve.wait_ge(r_in, 32)
            dve.wait_ge(routed, 1)
            dve.wait_ge(consts, NE)
            def wide(a):
                return a.unsqueeze(2).to_broadcast([P, RT, NE])

            ranks = rank[:].unsqueeze(1).to_broadcast([P, RT, NE])
            st.after(st(dve.tensor_tensor(lg[:], yb[:, 0, 0:RT * NE].rearrange("p (t n) -> p t n", n=NE),
                                          rb_row[:].unsqueeze(1).to_broadcast([P, RT, NE]), ALU.add)))

            def first_largest(values, largest, pick):
                st.after(st(dve.tensor_reduce(largest, values, AX, ALU.max)))
                st.after(st(dve.tensor_tensor(key[:], values, wide(largest), ALU.is_equal)))
                st.after(st(dve.tensor_tensor(key[:], key[:], ranks, ALU.mult)))
                st.after(st(dve.tensor_reduce(col[:, 3], key[:], AX, ALU.max)))
                st.after(st(dve.tensor_tensor(pick, key[:], wide(col[:, 3]), ALU.is_equal)))

            first_largest(lg[:], col[:, 0], pick1[:])
            st.after(st(dve.scalar_tensor_tensor(rest[:], pick1[:], -1e30, lg[:], ALU.mult, ALU.add)))
            first_largest(rest[:], col[:, 1], pick2[:])
            st.after(st(dve.tensor_tensor(pick1[:], pick1[:], pick2[:], ALU.add)))
            dve.tensor_tensor(lg[:], lg[:], wide(col[:, 0]), ALU.subtract).then_inc(gexp_in, 1)
            dve.wait_ge(gexp_out, 1)
            st.after(st(dve.tensor_tensor(lg[:], lg[:], pick1[:], ALU.mult)))
            st.after(st(dve.tensor_reduce(col[:, 2], lg[:], AX, ALU.add)))
            st.after(st(dve.reciprocal(col[:, 2], col[:, 2])))
            dve.tensor_tensor(lg[:], lg[:], wide(col[:, 2]), ALU.mult).then_inc(gates_out, 1)
            low_w13(1, 1)
            low_w2(0, 0)
            before = st.n

            def expert(n, turn, slot, ex, is_routed):
                dve.wait_ge(tanhd, n + 1)
                h1, h3 = (hid[:, j].rearrange("p c t -> p (c t)") for j in range(2))
                st.after(st(dve.scalar_tensor_tensor(th[:], th[:], 1.0, h1, ALU.add, ALU.mult)))
                if isinstance(n, int) and n == 0:
                    dve.wait_ge(gT_hi, 1)
                    dve.scalar_tensor_tensor(gT[:, 1], yb[0:NE, 1, :], GS, gT[:, 0], ALU.mult, ALU.subtract).then_inc(gT_lo, 1)
                if is_routed:
                    dve.tensor_tensor(th[:], th[:], h3, ALU.mult).then_inc(hid_read, 1)
                    dve.wait_ge(hid_read, n + 1)
                    gr = gate_row[:, bass.ds(ex, 1)].rearrange("p a t -> p (a t)").unsqueeze(1).to_broadcast([P, HH, ROWS])
                    dve.tensor_tensor(th[:].rearrange("p (c t) -> p c t", c=HH), th[:].rearrange("p (c t) -> p c t", c=HH),
                                      gr, ALU.mult).then_inc(g_f32, 1)
                else:
                    dve.scalar_tensor_tensor(th[:], th[:], 0.5 * GS / (WS * WS), h3, ALU.mult, ALU.mult).then_inc(hid_read, 1)
                    dve.wait_ge(hid_read, n + 1)
                    dve.nop().then_inc(g_f32, 1)
                if left(n, 1):
                    low_w2(n + 1, 1 - slot)
                dve.wait_ge(g_hi, n + 1)
                dve.tensor_tensor(gs[:, slot, 1], th[:].rearrange("p (c t) -> p c t", c=HH), gs[:, slot, 0],
                                  ALU.subtract).then_inc(g_lo, 1)
                if left(n, 2):
                    low_w13(n + 2, slot)

            def between(i):
                st.base, st.n = before + NS + 2 * i, 0

            experts_in_turn(dve, between, expert)
            for t in range(RT):
                dve.wait_ge(y_last, t + 1)
                dve.scalar_tensor_tensor(rows[:, t], yb[:, t, :], 1.0 / (WS * GS), rows[:, t], ALU.mult,
                                         ALU.add).then_inc(y_out, 1)

        @block.tensor
        def _(pe):
            for t in range(RT):
                pe.wait_ge(x_ready, t + 1)
                for dc in range(DC):
                    mm = pe.transpose(yb[:, t, dc * P:(dc + 1) * P], xn[:, t, dc * P:(dc + 1) * P], c.ident32[:])
                mm.then_inc(x_turned, 1)
            pe.wait_ge(x_out, RT)
            pe.wait_ge(r_in, 32)
            for t in range(RT):
                for dc in range(DC):
                    mm = pe.matmul(yb[:, 0, t * NE:(t + 1) * NE], xT[:, dc, t * P:(t + 1) * P], rw[:, dc],
                                   start=(dc == 0), stop=(dc == DC - 1))
            mm.then_inc(routed, 1)
            def hidden(n, slot):
                pe.wait_ge(w13_hi, n + 1)
                pe.wait_ge(w13_lo, n + 1)
                if not (isinstance(n, int) and n == 0):
                    pe.wait_ge(hid_read, n)
                for j in range(2):
                    for hc in range(HH):
                        k = 0
                        for dc in range(DC):
                            at = dc * HH * P + hc * P
                            for a, b in split_passes(lambda i: ws[:, slot, i, j, at:at + P], lambda i: xs[:, i, dc, :]):
                                mm = pe.matmul(hid[:, j, hc, :], a, b, start=(k == 0), stop=(k == 3 * DC - 1))
                                k += 1
                mm.then_inc(hid_done, 1)

            def down(n, slot, first, last):
                pe.wait_ge(w2_hi, n + 1)
                pe.wait_ge(w2_lo, n + 1)
                pe.wait_ge(g_hi, n + 1)
                pe.wait_ge(g_lo, n + 1)
                for t in range(RT):
                    k = 0
                    for hc in range(HH):
                        for a, b in split_passes(lambda i: gs[:, slot, i, hc, t * P:(t + 1) * P],
                                                 lambda i: ws[:, slot, i, 2, hc * D:(hc + 1) * D]):
                            mm = pe.matmul(yb[:, t, :], a, b, start=(first and k == 0), stop=(last and k == 5),
                                           skip_group_check=True)
                            k += 1
                    if last:
                        mm.then_inc(y_last, 1)
                if not last:
                    mm.then_inc(y_done, 1)

            pe.wait_ge(x_hi, 1)
            pe.wait_ge(x_lo, 1)
            hidden(0, 0)
            pe.wait_ge(gates_out, 1)
            for t in range(RT):
                mm = pe.transpose(yb[0:NE, 1, t * P:(t + 1) * P], lg[:, t], c.ident32[:])
            mm.then_inc(g_turned, 1)
            pe.wait_ge(gT_lo, 1)

            def spread_gates(n):
                if n >= RT:
                    pe.wait_ge(spread_out, n - RT + 1)
                for i in range(2):
                    mm = pe.matmul(yb[:, (n + 2) % RT, :], sel[:, n, :], gT[:, i], start=(i == 0), stop=(i == 1))
                mm.then_inc(spread, 1)

            for n in range(NE):
                spread_gates(n)
            hidden(1, 1)
            pe.wait_ge(spread_out, NE)
            down(0, 0, True, False)
            with pe.Fori(0, NE // 2) as i:
                for u in range(2):
                    n = NS + 2 * i + u
                    hidden(n, u)
                    down(n - 1, (u + 1) % 2, False, False)
            down(NS + NE - 1, 1, False, True)


class Named:
    pass


def perceiver_kernel(nc, x, ctx_1024, Wq, Wk, Wv, gru_wih, gru_whh, gru_bih, gru_bhh, slot_norm_w, input_norm_w,
                     Wqkv, bqkv, Wo, bo, router_w, router_b, routed_w1, routed_w3, routed_w2,
                     shared_w1, shared_w3, shared_w2, out):
    dram = Named()
    dram.x, dram.ctx, dram.Wq, dram.Wk, dram.Wv = x, ctx_1024, Wq, Wk, Wv
    dram.gru_wih, dram.gru_whh, dram.gru_bih, dram.gru_bhh = gru_wih, gru_whh, gru_bih, gru_bhh
    dram.slot_norm_w, dram.input_norm_w = slot_norm_w, input_norm_w
    dram.Wqkv, dram.bqkv, dram.Wo, dram.bo = Wqkv, bqkv, Wo, bo
    dram.router_w, dram.router_b = router_w, router_b
    dram.routed, dram.shared = (routed_w1, routed_w3, routed_w2), (shared_w1, shared_w3, shared_w2)
    with ExitStack() as ctx:
        def sb(name, shape, dt):
            return ctx.enter_context(nc.sbuf_tensor(name, shape, dt))

        def sem(name):
            return ctx.enter_context(nc.semaphore(name))

        c = Named()
        c.ident32, c.ident16 = sb("ident32", [P, P], F32), sb("ident16", [P, P], F16)
        c.ones32 = sb("ones32", [P, P], F32)
        c.b_rz, c.b_n = sb("b_rz", [P, 2 * DC], F32), sb("b_n", [P, 2 * DC], F32)
        slots = sb("slots", [P, RT, DC, P], F32)
        rows = sb("rows", [P, RT, D], F32)
        big = Named()
        big.ctxT = [sb(f"ctxT{n}", [P, MT, 2, DC, P], F16) for n in range(2)]
        big.tail = [sb(f"tail{n}", [P, D], F32) for n in range(2)]
        big.ctx_in = [[sem(f"ctx_in{g}_{n}") for n in range(2)] for g in range(2)]
        big.ssq = [sb(f"ssq{n}", [P, MT], F32) for n in range(2)]
        big.squares = [sem(f"squares{n}") for n in range(2)]
        big.wqkv_in = sem("wqkv_in")
        big.x_in = sem("x_again_in")
        e = Named()
        e.raw = words(big.ctxT[1])[:, 0:6 * 1024].rearrange("p (s j n) -> p s j n", s=2, j=3)
        e.stats = sb("e_stats", [P, RT, 6], F32)
        e.mv = sb("e_mv", [P, RT, 2], F32)
        e.w13_in = [sem(f"w13_in{slot}") for slot in range(2)]
        e.w2_in = [sem(f"w2_in{slot}") for slot in range(2)]
        with ExitStack() as inner:
            w = Named()
            w.A = inner.enter_context(nc.sbuf_tensor("A", [P, 2, DC, D], F16))
            w.Bt = inner.enter_context(nc.sbuf_tensor("Bt", [P, 2, DC, G3], F16))
            w.whhT = inner.enter_context(nc.sbuf_tensor("whhT", [P, 2, DC, G3], F16))
            prepare_weights(nc, w, c, dram, slots, rows, big)
            slot_attention(nc, w, c, dram, slots, rows, big, e)
        with ExitStack() as inner:
            folded = [inner.enter_context(nc.sbuf_tensor(name, [P, HC, ROWS], F32)) for name in ("qT", "kT", "vT")]
            wqkvT = folded[2][:].rearrange("p c t -> p (c t)").bitcast(F16)[:, 0:2 * DC * G3]\
                .rearrange("p (s c g) -> p s c g", s=2, c=DC)
            folded = [f[0:HD] for f in folded]
            woT = inner.enter_context(nc.sbuf_tensor("woT", [P, 2, DC, D], F16))
            project_qkv(nc, c, dram, slots, rows, folded, wqkvT, woT, big)
            head_attention(nc, c, dram, slots, rows, folded, woT, big, e)
        experts(nc, c, dram, rows, out, e)


_INS = ['x', 'ctx_1024', 'L0_xattn_Wq', 'L0_xattn_Wk', 'L0_xattn_Wv', 'L0_xattn_gru_wih', 'L0_xattn_gru_whh',
        'L0_xattn_gru_bih', 'L0_xattn_gru_bhh', 'L0_xattn_slot_norm_w', 'L0_xattn_input_norm_w', 'L0_attn_Wqkv',
        'L0_attn_bqkv', 'L0_attn_Wo', 'L0_attn_bo', 'L0_ffn_router_w', 'L0_ffn_router_b', 'L0_ffn_routed_w1',
        'L0_ffn_routed_w3', 'L0_ffn_routed_w2', 'L0_ffn_shared_w1', 'L0_ffn_shared_w3', 'L0_ffn_shared_w2']
_OUTS = [((8, 64, 512), 'float32')]


def kernel(**inputs):
    import numpy as _np
    import concourse.bacc as _bacc
    from concourse import mybir as _mybir
    from concourse.bass_utils import run_bass_kernel_spmd as _run

    nc = _bacc.Bacc("TRN2", target_bir_lowering=False, num_devices=1)
    arrays, args = {}, []
    for name in _INS:
        a = _np.ascontiguousarray(inputs[name])
        arrays[f"in_{name}_dram"] = a
        args.append(nc.dram_tensor(f"in_{name}_dram", a.shape, _mybir.dt.from_np(a.dtype), kind="ExternalInput").ap())
    for i, (shape, dtype) in enumerate(_OUTS):
        dt = _mybir.dt.from_np(_np.dtype(dtype))
        args.append(nc.dram_tensor(f"out_{i}_dram", shape, dt, kind="ExternalOutput").ap())
    perceiver_kernel(nc, *args)
    r = _run(nc, [arrays], core_ids=[0])
    got = tuple(r.results[0][f"out_{i}_dram"] for i in range(len(_OUTS)))
    return got[0]
```
